# Optimizing a Trainium2 kernel written in Bass

```python
import numpy as np
import jax
import jax.numpy as jnp

def _softmax(x, axis=-1):
    return jax.nn.softmax(x, axis=axis)

def _gelu(x):
    return jax.nn.gelu(x, approximate=True)

def _silu(x):
    return jax.nn.silu(x)

def _sigmoid(x):
    return jax.nn.sigmoid(x)

def _layernorm(x, axis=-1, eps=1e-05):
    m = jnp.mean(x, axis=axis, keepdims=True)
    v = jnp.var(x, axis=axis, keepdims=True)
    return (x - m) / jnp.sqrt(v + eps)

def _scatter_add(tgt, idx, src, axis=0):
    return tgt.at[idx].add(src)

def _segment_sum(src, seg, n):
    return jax.ops.segment_sum(src, seg, n)
kernel_name = 'mk_cond_resid_d2_seqx_r8_0d1b16'

def setup_inputs(seed: int=0):
    np.random.seed(seed)
    _w = jnp.asarray

    def _rec_inputs():
        import jax
        import jax.numpy as jnp
        _rk = jax.random.key(seed)
        x = -0.0005207 + 1.001 * jax.random.normal(jax.random.fold_in(_rk, 1), (8, 128, 512), jnp.float32)
        _lenS = 128 - jax.random.randint(jax.random.fold_in(_rk, 7), (8,), 0, max(1, 128 // 4) + 1, jnp.int32)
        _lenS2 = 128 - jax.random.randint(jax.random.fold_in(_rk, 8), (8,), 0, max(1, 128 // 4) + 1, jnp.int32)
        itok_Bx16_0_63 = jax.random.randint(jax.random.fold_in(_rk, 11), (8, 16), 0, 64, jnp.int32)
        itok_B_207_1644 = jax.random.randint(jax.random.fold_in(_rk, 12), (8,), 207, 1645, jnp.int32)
        itok_B_0_7 = jax.random.randint(jax.random.fold_in(_rk, 13), (8,), 0, 8, jnp.int32)
        return (x, itok_Bx16_0_63, itok_B_207_1644, itok_B_0_7)
    x, itok_Bx16_0_63, itok_B_207_1644, itok_B_0_7 = _rec_inputs()

    def _L0_cond_setup():
        import jax, jax.numpy as jnp
        import numpy as np
        B, S, HID = (4, 128, 512)
        D, HQ, HK = (128, 32, 8)
        PAGES, PSIZE, NPP = (64, 32, 16)
        THETA = 10000.0
        EPS = 1e-06
        SCALE = 1.0 / float(np.sqrt(D))

        def _rmsnorm(t, w):
            var = jnp.mean(t * t, axis=-1, keepdims=True)
            return t * jax.lax.rsqrt(var + EPS) * w

        def _rope(t, pos):
            inv_freq = 1.0 / THETA ** (jnp.arange(0, D, 2, dtype=jnp.float32) / D)
            freqs = pos[..., None].astype(jnp.float32) * inv_freq
            cos = jnp.cos(freqs)[:, :, None, :]
            sin = jnp.sin(freqs)[:, :, None, :]
            t1, t2 = (t[..., :D // 2], t[..., D // 2:])
            return jnp.concatenate([t1 * cos - t2 * sin, t2 * cos + t1 * sin], axis=-1)
        key = jax.random.key(seed)
        ks = jax.random.split(key, 10)
        x = jax.random.normal(ks[0], (B, S, HID), jnp.float32)
        Wq = jax.random.normal(ks[1], (HQ * D, HID), jnp.float32) * 0.02
        Wk = jax.random.normal(ks[2], (HK * D, HID), jnp.float32) * 0.02
        Wv = jax.random.normal(ks[3], (HK * D, HID), jnp.float32) * 0.02
        Wo = jax.random.normal(ks[4], (HID, HQ * D), jnp.float32) * 0.02
        q_norm_w = jax.random.uniform(ks[5], (D,), jnp.float32)
        k_norm_w = jax.random.uniform(ks[6], (D,), jnp.float32)
        k_cache = jax.random.normal(ks[7], (PAGES, PSIZE, HK, D), jnp.float32)
        v_cache = jax.random.normal(ks[8], (PAGES, PSIZE, HK, D), jnp.float32)
        block_table = jnp.arange(B * NPP, dtype=jnp.int32).reshape(B, NPP)
        cache_seqlens = jax.random.randint(ks[9], (B,), 0, 475).astype(jnp.int32)
        return dict(x=x, Wq=Wq, Wk=Wk, Wv=Wv, Wo=Wo, q_norm_w=q_norm_w, k_norm_w=k_norm_w, k_cache=k_cache, v_cache=v_cache, block_table=block_table, cache_seqlens=cache_seqlens)
    _L0_cond_all = _L0_cond_setup()
    _L0_cond_in = {k: v for k, v in _L0_cond_all.items() if k in ('Wq', 'Wk', 'Wv', 'Wo', 'q_norm_w', 'k_norm_w', 'k_cache', 'v_cache')}
    del _L0_cond_all

    def _L1_cond_setup():
        import jax, jax.numpy as jnp
        import numpy as np
        TOP_K = 2
        LANG_BIAS = 5.0
        SCALING = 32.0 / 16.0
        LANGUAGE_PAD_ID = -1
        key = jax.random.key(seed)
        ks = jax.random.split(key, 6)
        B, T, D, O, E, R = (4, 256, 512, 512, 8, 16)
        x = jax.random.normal(ks[0], (B, T, D), dtype=jnp.float32)
        language_ids = jax.random.randint(ks[1], (B,), 0, E).astype(jnp.int64)
        W = jax.random.normal(ks[2], (O, D), dtype=jnp.float32) * (1.0 / np.sqrt(D))
        Wr = jax.random.normal(ks[3], (E, D), dtype=jnp.float32) * (1.0 / np.sqrt(D))
        A = jax.random.normal(ks[4], (E, R, D), dtype=jnp.float32) * (1.0 / np.sqrt(D))
        Bm = jax.random.normal(ks[5], (O, R), dtype=jnp.float32) * 0.0
        Bm = jnp.broadcast_to(Bm, (E, O, R)) + jax.random.normal(ks[5], (E, O, R), dtype=jnp.float32) * 0.02
        return {'x': x, 'language_ids': language_ids, 'W': W, 'Wr': Wr, 'A': A, 'B': Bm}
    _L1_cond_all = _L1_cond_setup()
    _L1_cond_in = {k: v for k, v in _L1_cond_all.items() if k in ('W', 'Wr', 'A', 'B')}
    del _L1_cond_all
    return {'x': x, 'itok_Bx16_0_63': itok_Bx16_0_63, 'itok_B_207_1644': itok_B_207_1644, 'itok_B_0_7': itok_B_0_7, 'L0_cond_Wq': _L0_cond_in['Wq'], 'L0_cond_Wk': _L0_cond_in['Wk'], 'L0_cond_Wv': _L0_cond_in['Wv'], 'L0_cond_Wo': _L0_cond_in['Wo'], 'L0_cond_q_norm_w': _L0_cond_in['q_norm_w'], 'L0_cond_k_norm_w': _L0_cond_in['k_norm_w'], 'L0_cond_k_cache': _L0_cond_in['k_cache'], 'L0_cond_v_cache': _L0_cond_in['v_cache'], 'L1_cond_W': _L1_cond_in['W'], 'L1_cond_Wr': _L1_cond_in['Wr'], 'L1_cond_A': _L1_cond_in['A'], 'L1_cond_B': _L1_cond_in['B']}

def reference(x, itok_Bx16_0_63, itok_B_207_1644, itok_B_0_7, L0_cond_Wq, L0_cond_Wk, L0_cond_Wv, L0_cond_Wo, L0_cond_q_norm_w, L0_cond_k_norm_w, L0_cond_k_cache, L0_cond_v_cache, L1_cond_W, L1_cond_Wr, L1_cond_A, L1_cond_B):
    import jax
    import jax.numpy as jnp

    def _L0_cond_ref(x, Wq, Wk, Wv, Wo, q_norm_w, k_norm_w, k_cache, v_cache, block_table, cache_seqlens):
        import jax, jax.numpy as jnp
        import numpy as np
        B, S, HID = (4, 128, 512)
        D, HQ, HK = (128, 32, 8)
        PAGES, PSIZE, NPP = (64, 32, 16)
        THETA = 10000.0
        EPS = 1e-06
        SCALE = 1.0 / float(np.sqrt(D))

        def _rmsnorm(t, w):
            var = jnp.mean(t * t, axis=-1, keepdims=True)
            return t * jax.lax.rsqrt(var + EPS) * w

        def _rope(t, pos):
            inv_freq = 1.0 / THETA ** (jnp.arange(0, D, 2, dtype=jnp.float32) / D)
            freqs = pos[..., None].astype(jnp.float32) * inv_freq
            cos = jnp.cos(freqs)[:, :, None, :]
            sin = jnp.sin(freqs)[:, :, None, :]
            t1, t2 = (t[..., :D // 2], t[..., D // 2:])
            return jnp.concatenate([t1 * cos - t2 * sin, t2 * cos + t1 * sin], axis=-1)
        bsz, seqlen, _ = x.shape
        q = jnp.einsum('bsd,ed->bse', x, Wq).reshape(bsz, seqlen, HQ, D)
        k = jnp.einsum('bsd,ed->bse', x, Wk).reshape(bsz, seqlen, HK, D)
        v = jnp.einsum('bsd,ed->bse', x, Wv).reshape(bsz, seqlen, HK, D)
        q = _rmsnorm(q, q_norm_w)
        k = _rmsnorm(k, k_norm_w)
        pos = cache_seqlens[:, None] + jnp.arange(seqlen)[None, :]
        q = _rope(q, pos)
        k = _rope(k, pos)
        L = NPP * PSIZE
        kc = k_cache[block_table].reshape(bsz, L, HK, D)
        vc = v_cache[block_table].reshape(bsz, L, HK, D)
        k_all = jnp.concatenate([kc, k], axis=1)
        v_all = jnp.concatenate([vc, v], axis=1)
        valid_c = jnp.arange(L)[None, :] < cache_seqlens[:, None]
        valid = jnp.concatenate([valid_c, jnp.ones((bsz, seqlen), dtype=bool)], axis=1)
        rep = HQ // HK
        k_all = jnp.repeat(k_all, rep, axis=2)
        v_all = jnp.repeat(v_all, rep, axis=2)
        scores = jnp.einsum('bqhd,bkhd->bhqk', q, k_all) * SCALE
        scores = jnp.where(valid[:, None, None, :], scores, -1e+30)
        probs = jax.nn.softmax(scores, axis=-1)
        o = jnp.einsum('bhqk,bkhd->bqhd', probs, v_all)
        o = o.reshape(bsz, seqlen, HQ * D)
        return jnp.einsum('bse,de->bsd', o, Wo)

    def _L1_cond_ref(x, language_ids, W, Wr, A, B):
        import jax, jax.numpy as jnp
        import numpy as np
        TOP_K = 2
        LANG_BIAS = 5.0
        SCALING = 32.0 / 16.0
        LANGUAGE_PAD_ID = -1
        base = jnp.einsum('btd,od->bto', x, W)
        E = Wr.shape[0]
        logits = jnp.einsum('btd,ed->bte', x.astype(jnp.float32), Wr.astype(jnp.float32))
        expert_targets = language_ids
        valid = expert_targets >= 0
        tgt = jnp.where(valid, expert_targets, 0)
        bias = jax.nn.one_hot(tgt, E, dtype=logits.dtype) * LANG_BIAS
        bias = jnp.where(valid[:, None], bias, 0.0)
        logits = logits + bias[:, None, :]
        topw, topi = jax.lax.top_k(logits, TOP_K)
        weights = jax.nn.softmax(topw, axis=-1)
        gates = jnp.sum(jax.nn.one_hot(topi, E, dtype=weights.dtype) * weights[..., None], axis=-2)
        gates = gates.astype(x.dtype)
        h = jnp.einsum('btd,erd->bter', x, A)
        lora_out = jnp.einsum('bter,bte,eor->bto', h, gates, B)
        return base + SCALING * lora_out
    x = x + _L0_cond_ref(x, L0_cond_Wq, L0_cond_Wk, L0_cond_Wv, L0_cond_Wo, L0_cond_q_norm_w, L0_cond_k_norm_w, L0_cond_k_cache, L0_cond_v_cache, itok_Bx16_0_63, itok_B_207_1644)
    x = x + _L1_cond_ref(x, itok_B_0_7, L1_cond_W, L1_cond_Wr, L1_cond_A, L1_cond_B)
    return x

_drawn_inputs = setup_inputs


def setup_inputs(seed=0):
    import zlib

    import numpy as np

    out = dict(_drawn_inputs(seed))
    spreads = {}
    factors = {'L0_cond_Wk': 8.0,
     'L0_cond_Wv': 31.965,
     'L0_cond_q_norm_w': 2.873,
     'L0_cond_k_norm_w': 21.948,
     'L1_cond_Wr': 5.5,
     'L0_cond_k_cache': 8.0,
     'L0_cond_v_cache': 8.0}
    for name, (base, spread) in spreads.items():
        noise = np.random.default_rng([zlib.crc32(name.encode()), seed]).standard_normal(out[name].shape)
        drawn = base * np.exp(spread * noise) if base else spread * noise
        out[name] = jnp.asarray(drawn.astype(out[name].dtype))
    for name, factor in factors.items():
        out[name] = (out[name] * factor).astype(out[name].dtype)
    return out
```

```python
from contextlib import ExitStack

import numpy as np
import concourse.bass as bass
from concourse import mybir

F32 = mybir.dt.float32
F32R = mybir.dt.float32r
BF16 = mybir.dt.bfloat16
I32 = mybir.dt.int32
U32 = mybir.dt.uint32
ALU = mybir.AluOpType
ACT = mybir.ActivationFunctionType
AX_X = mybir.AxisListType.X

P = 128
B = 8
S = 128
HID = 512
D = 128
HALF = D // 2
HK = 8
REP = 4
HQ = HK * REP
PAGES, PSIZE, NPP = 64, 32, 16
L = PSIZE * NPP
KEYS = L + S
KT = KEYS // P
CT = L // P
KC = HID // P
QW = REP * D
WW = QW + 2 * D
NH = REP + 1
G = HK * B
E, R = 8, 16
ER = E * R
WL = HID + ER + E
SCALE = 1.0 / float(np.sqrt(D))
NORM_EPS = 1e-6
MASKED = -1e30
LANG_BIAS = 5.0
LORA_SCALING = 32.0 / 16.0
THETA = 10000.0

C_INVF = 0
C_IDENT = C_INVF + HALF
C_EXPERT = C_IDENT + P
C_ROW = C_EXPERT + E
C_SLOT = C_ROW + 1
C_END = C_SLOT + 1
I_BLOCK = 0
I_LEN = I_BLOCK + B * CT
I_LANG = I_LEN + B
I_END = I_LANG + B

TWO_PI = 2.0 * np.pi
TWO_PI_A = 6.28125
TWO_PI_B = float(np.float32(int((TWO_PI - TWO_PI_A) * 2**20) / 2**20))
TWO_PI_C = float(np.float32(TWO_PI - TWO_PI_A - TWO_PI_B))
PI_BELOW = 3.1415925

UNITS = ["R", "O", "T0", "Q", "T1", "Y", "QT", "KTC", "KTN", "T2", "KV", "T3", "TN"]
NU = len(UNITS)
NBANK = 4


def attention_lora(nc, xT, x, wqkv, wo, kv, normw, kpos, consts, ints, w1, wB, out):
    with ExitStack() as ctx:
        def sb(name, shape, dt=F32):
            return ctx.enter_context(nc.sbuf_tensor(name, shape, dt))

        def sem(name):
            return ctx.enter_context(nc.semaphore(name))

        xt_hi, xt_lo = sb("xt_hi", [P, KC, B * S], F32R), sb("xt_lo", [P, KC, B * S], F32R)
        w_raw = sb("w_raw", [P, KC * WW])
        w_hi, w_lo = sb("w_hi", [P, KC * WW], F32R), sb("w_lo", [P, KC * WW], F32R)
        wo_raw = sb("wo_raw", [P, REP * HID])
        wo_hi, wo_lo = sb("wo_hi", [P, REP * HID], F32R), sb("wo_lo", [P, REP * HID], F32R)
        kv_raw = sb("kv_raw", [P, 2, CT, 2 * D])
        y = sb("y", [P, B, HID])
        mask = sb("mask", [P, B, KEYS], BF16)
        cos = sb("cos", [P, B, HALF])
        sin = sb("sin", [P, B, D])
        cst = sb("cst", [P, C_END])
        cin = sb("cin", [P, I_END], I32)
        nw = sb("nw", [P, NH, D])
        raw = sb("raw", [P, 2, WW])
        wr = sb("wr", [P, NH, D])
        u = sb("u", [P, NH, D])
        rot = sb("rot", [P, NH, D])
        m2 = sb("m2", [P, NH, D])
        qt_hi, qt_lo = sb("qt_hi", [P, QW], F32R), sb("qt_lo", [P, QW], F32R)
        kt_hi, kt_lo = sb("kt_hi", [P, KEYS], F32R), sb("kt_lo", [P, KEYS], F32R)
        v_hi, v_lo = sb("v_hi", [P, KT, D], F32R), sb("v_lo", [P, KT, D], F32R)
        ps = sb("ps", [P, REP, KEYS])
        pt_hi, pt_lo = sb("pt_hi", [P, KT, REP, S], F32R), sb("pt_lo", [P, KT, REP, S], F32R)
        rb = sb("rb", [P, REP * S])
        on = sb("on", [P, REP * S])
        o_hi, o_lo = sb("o_hi", [P, REP * S], F32R), sb("o_lo", [P, REP * S], F32R)
        negmax = sb("negmax", [P, 2, REP])
        rowsum = sb("rowsum", [P, 2, REP])
        recip = sb("recip", [P, 2, REP])
        sumsq = sb("sumsq", [P, NH])
        meansq = sb("meansq", [P, NH])
        rstd = sb("rstd", [P, NH])
        mhalf = sb("mhalf", [P, NH])
        pos = sb("pos", [P, B])
        lenf = sb("lenf", [P, B])
        langf = sb("langf", [P, B])
        halfpi = sb("halfpi", [P, 1])
        blkf = sb("blkf", [P, B, CT])
        rows = sb("rows", [P, B, CT], I32)
        lang_bias = sb("lang_bias", [P, B, E])
        logits = sb("logits", [P, B, E])
        top = sb("top", [P, B, 8])
        topi = sb("topi", [P, B, 8], U32)
        topf = sb("topf", [P, B, 2])
        gd = sb("gd", [P, B])
        ge = sb("ge", [P, B])
        gs = sb("gs", [P, B])
        gw = sb("gw", [P, 2, B])
        gate = sb("gate", [P, 2, B, E])

        ident = cst[:, C_IDENT:C_IDENT + P]
        wh = w_hi[:].rearrange("p (k n) -> p k n", k=KC)
        wl = w_lo[:].rearrange("p (k n) -> p k n", k=KC)
        wrw = w_raw[:].rearrange("p (k n) -> p k n", k=KC)
        ps_s = ctx.enter_context(nc.psum_tensor("ps_s", [P, 2, 1024], F32))
        ps_w = ctx.enter_context(nc.psum_tensor("ps_w", [P, NBANK, 512], F32))

        s_x0, s_x1, s_cst, s_y, s_out = sem("x0_landed"), sem("x1_landed"), sem("consts_landed"), sem("y_landed"), [sem("out_stored0"), sem("out_stored1")]
        s_wraw, s_woraw = sem("wqkv_landed"), sem("wo_landed")
        s_kv = [sem("kv0_landed"), sem("kv1_landed")]
        pe_q, pe_kv, pe_qt, pe_ktc, pe_ktn = sem("pe_q"), sem("pe_kv"), sem("pe_qt"), sem("pe_ktc"), sem("pe_ktn")
        pe_s, pe_t, pe_tn, pe_r, pe_o, pe_y = sem("pe_s"), sem("pe_t"), sem("pe_tn"), sem("pe_r"), sem("pe_o"), sem("pe_y")
        pe_xt, pe_ar, pe_ht, pe_out = sem("pe_xt"), sem("pe_ar"), sem("pe_ht"), sem("pe_out")
        a_xhi, a_whi, a_wohi = sem("a_xhi"), sem("a_whi"), sem("a_wohi")
        a_sincos, a_exp, a_q, a_kv, a_sq = sem("a_sincos"), sem("a_exp"), sem("a_q"), sem("a_kv"), sem("a_sq")
        a_qt, a_ktc, a_ktn, a_pt, a_r, a_o = sem("a_qt"), sem("a_ktc"), sem("a_ktn"), sem("a_pt"), sem("a_r"), sem("a_o")
        a_h, a_ge, a_ht = sem("a_h"), sem("a_ge"), sem("a_ht")
        d_tab, d_xlo, d_wlo, d_wolo, d_rows = sem("d_tab"), sem("d_xlo"), sem("d_wlo"), sem("d_wolo"), sem("d_rows")
        d_mask, d_ang, d_ss, d_u, d_m2 = sem("d_mask"), sem("d_ang"), sem("d_ss"), sem("d_u"), sem("d_m2")
        d_qt, d_ktc, d_ktn, d_max, d_pt = sem("d_qt"), sem("d_ktc"), sem("d_ktn"), sem("d_max"), sem("d_pt")
        d_recip, d_on, d_olo, d_y = sem("d_recip"), sem("d_on"), sem("d_olo"), sem("d_y")
        d_gate, d_lg, d_gd, d_hg, d_ht, d_fin = sem("d_gate"), sem("d_lg"), sem("d_gd"), sem("d_hg"), sem("d_ht"), sem("d_fin")
        d_mark, p_mark = sem("d_mark"), sem("p_mark")
        p_init, p_ms, p_rstd, p_wr, p_m1, p_rot = sem("p_init"), sem("p_ms"), sem("p_rstd"), sem("p_wr"), sem("p_m1"), sem("p_rot")
        p_vhi, p_v, p_rows = sem("p_vhi"), sem("p_v"), sem("p_rows")

        def has(i, off):
            return not isinstance(i, int) or 0 <= i + off < G

        def wait(eng, s, i, off, per=1, nth=None):
            add = off * per + (per if nth is None else nth)
            if isinstance(i, int):
                if i + off >= 0:
                    eng.wait_ge(s, i * per + add)
            else:
                eng.wait_ge(s, (i if per == 1 else i * per) + add)

        def carry(eng, i, mark):
            if not isinstance(i, int):
                eng.sem_inc(mark, 1)

        def wait_kv(eng, i, off):
            eng.wait_ge(s_kv[off % 2], i * 32 + 64 * (off // 2 + 1))

        def bank(b, unit):
            return ps_w[:, (NU * b + UNITS.index(unit)) % NBANK, :]

        FREES = {"R": (a_r, 1, 1, -1), "O": (d_on, 1, 1, -1), "T0": (d_pt, 5, 1, 0), "Q": (a_q, 1, 1, 2),
                 "T1": (d_pt, 5, 2, 0), "Y": (d_y, 1, 1, -1), "QT": (d_qt, 1, 1, 1), "KTC": (d_ktc, 1, 1, 1),
                 "KTN": (d_ktn, 1, 1, 1), "T2": (d_pt, 5, 3, 0), "KV": (a_kv, 1, 1, 2), "T3": (d_pt, 5, 4, 0),
                 "TN": (d_pt, 5, 5, 0)}

        def wait_bank(pe, i, b, unit):
            n = UNITS.index(unit)
            while True:
                n -= NBANK
                if n < 0:
                    n, b = n + NU, b - 1
                if b < -2:
                    return
                s, per, nth, off = FREES[UNITS[n]]
                if has(i, b + off):
                    wait(pe, s, i, b + off, per, nth)
                    return

        def three_passes(out_ap, pairs, start=True, stop=True):
            n = len(pairs)
            last = None
            for k, (a_hi, a_lo, b_hi, b_lo) in enumerate(pairs):
                nc.tensor.matmul(out_ap, a_hi, b_hi, start=start and k == 0, stop=False)
                nc.tensor.matmul(out_ap, a_hi, b_lo, start=False, stop=False)
                last = nc.tensor.matmul(out_ap, a_lo, b_hi, start=False, stop=stop and k == n - 1)
            return last


        def expert_bank(b):
            return ps_s[:, b % 2, b // 2 % 2 * 512:b // 2 % 2 * 512 + ER + E]

        hflat = ps[:].rearrange("p h k -> p (h k)")

        block = ctx.enter_context(nc.Block())

        @block.sync
        def _(sp):
            sp.dma_start(wo_raw[:], xT[0]).then_inc(s_x0, 16)
            sp.dma_start(w_raw[:], wqkv[0]).then_inc(s_wraw, 16)
            sp.dma_start(cin[:], ints[:, :]).then_inc(s_cst, 16)
            sp.dma_start(cst[:], consts[:, :]).then_inc(s_cst, 16)
            sp.dma_start(nw[:].rearrange("p h d -> p (h d)"), normw[:, :]).then_inc(s_cst, 16)
            sp.dma_start(rot[:].rearrange("p h d -> p (h d)"), kpos[:, :]).then_inc(s_cst, 16)
            sp.wait_ge(d_xlo, B // 2)
            sp.dma_start(wo_raw[:], xT[1]).then_inc(s_x1, 16)
            sp.dma_start(y[:], x.rearrange("b s h -> s b h")).then_inc(s_y, 16)
            sp.wait_ge(d_xlo, B)
            sp.dma_start(wo_raw[:], wo[0]).then_inc(s_woraw, 16)

            def next_weights(h):
                sp.wait_ge(d_wlo, h * 5)
                sp.dma_start(w_raw[:], wqkv[h]).then_inc(s_wraw, 16)
                sp.wait_ge(d_wolo, h * 4)
                sp.dma_start(wo_raw[:], wo[h]).then_inc(s_woraw, 16)

            with sp.Fori(1, HK) as h:
                next_weights(h)
            sp.wait_ge(d_wlo, HK * 5)
            sp.dma_start(w_raw[:, 0:KC * WL], w1[:, :]).then_inc(s_wraw, 16)
            sp.wait_ge(d_wolo, HK * 4)
            sp.dma_start(wo_raw[:, 0:HID], wB[:, :]).then_inc(s_woraw, 16)
            for b in range(B):
                sp.wait_ge(d_fin, b + 1)
                sp.dma_start(out[b], (rb if b % 2 else on)[:]).then_inc(s_out[b % 2], 16)
            for stored in s_out:
                sp.wait_ge(stored, 16 * B // 2)

        @block.gpsimd
        def _(pool):
            nc.gpsimd.memset(mhalf[:], -0.5).then_inc(p_init, 1)

            def gather(b):
                pool.wait_ge(d_rows, 1)
                nc.gpsimd.tensor_scalar(rows[:, b % B, :], rows[:, b % B, :], float(PAGES * PSIZE), None,
                                        ALU.add).then_inc(p_rows, 1)

            def gather_dma(i, b):
                wait(pool, p_rows, i, b)
                wait(pool, pe_ktc, i, b - 2)
                wait(pool, p_v, i, b - 2, 2)
                carry(pool, i, p_mark)
                for t in range(CT):
                    pool.indirect_dma_start(kv_raw[:, b % 2, t, :], None, kv[:, :],
                                            bass.IndirectOffsetOnAxis(rows[:, b % B, t:t + 1], 0)
                                            ).then_inc(s_kv[b % 2], 16)

            def step(i, b):
                g1 = b + 1
                if has(i, g1):
                    wait(pool, d_ss, i, g1)
                    carry(pool, i, p_mark)
                    nc.gpsimd.tensor_scalar(meansq[:], sumsq[:], 1.0 / D, NORM_EPS, ALU.mult, ALU.add).then_inc(p_ms, 1)
                    wait(pool, p_ms, i, g1)
                    nc.gpsimd.tensor_tensor(rstd[:], meansq[:], mhalf[:], ALU.pow).then_inc(p_rstd, 1)
                    wait(pool, p_rstd, i, g1)
                    wait(pool, d_u, i, g1 - 1)
                    nc.gpsimd.tensor_tensor(wr[:], nw[:], rstd[:].unsqueeze(2).to_broadcast([P, NH, D]),
                                            ALU.mult).then_inc(p_wr, 1)
                    wait(pool, d_u, i, g1)
                    wait(pool, pe_ktn, i, g1 - 1)
                    nc.gpsimd.tensor_tensor(rot[:].rearrange("p h (t d) -> p (h t) d", t=2),
                                            u[:].rearrange("p h (t d) -> p (h t) d", t=2),
                                            cos[:, g1 % B, :].unsqueeze(1).to_broadcast([P, 2 * NH, HALF]),
                                            ALU.mult).then_inc(p_m1, 1)
                    wait(pool, p_m1, i, g1)
                    wait(pool, d_m2, i, g1)
                    for a, c in ((0, HALF), (HALF, 0)):
                        nc.gpsimd.tensor_tensor(rot[:, :, a:a + HALF], rot[:, :, a:a + HALF],
                                                m2[:, :, c:c + HALF], ALU.add).then_inc(p_rot, 1)
                if has(i, b):
                    wait_kv(pool, i, b)
                    wait(pool, a_kv, i, b)
                    wait(pool, pe_o, i, b - 1)
                    carry(pool, i, p_mark)
                    cached, new = kv_raw[:, b % 2, :, D:2 * D], raw[:, b % 2, QW + D:WW]
                    nc.gpsimd.tensor_copy(v_hi[:, 0:CT, :], cached).then_inc(p_vhi, 1)
                    nc.gpsimd.tensor_copy(v_hi[:, CT, :], new).then_inc(p_vhi, 1)
                    wait(pool, p_vhi, i, b, 2)
                    nc.gpsimd.tensor_tensor(v_lo[:, 0:CT, :], cached, v_hi[:, 0:CT, :].bitcast(F32), ALU.subtract).then_inc(p_v, 1)
                    nc.gpsimd.tensor_tensor(v_lo[:, CT, :], new, v_hi[:, CT, :].bitcast(F32), ALU.subtract).then_inc(p_v, 1)
                    if has(i, b + 2):
                        gather(b + 2)
                        gather_dma(i, b + 2)

            pool.wait_ge(d_rows, 1)
            for b in range(2):
                gather(b)
            for b in range(2):
                gather_dma(0, b)
            pool.wait_ge(s_cst, 64)
            pool.wait_ge(a_sincos, 2)
            pool.wait_ge(d_tab, 1)
            pool.wait_ge(d_mask, B)
            pool.wait_ge(p_init, 1)
            for b in range(-2, B):
                step(0, b)
            with pool.Fori(B, G - B, B) as i:
                for b in range(B):
                    step(i, b)
            for b in range(B + 1):
                step(G - B, b)

        @block.scalar
        def _(act):
            def split_w(i, b, k0, k1, cols):
                c0, c1 = cols
                return nc.scalar.activation(wh[:, k0:k1, c0:c1], wrw[:, k0:k1, c0:c1], ACT.Copy)

            def step(i, b):
                g1, g2 = b + 1, b + 2
                if has(i, g1):
                    wait(act, pe_kv, i, g1)
                    wait(act, p_v, i, g1 - 2, 2)
                    wait(act, d_u, i, g1 - 2)
                    nc.scalar.activation(raw[:, g1 % 2, QW:WW], bank(b - 1, "KV")[:, 0:2 * D], ACT.Copy).then_inc(a_kv, 1)
                    wait(act, a_kv, i, g1)
                    wait(act, a_q, i, g1)
                    wait(act, d_m2, i, g1 - 1)
                    wait(act, p_m1, i, g1 - 1)
                    nc.scalar.activation(u[:].rearrange("p h d -> p (h d)"), raw[:, g1 % 2, 0:QW + D], ACT.Square).then_inc(a_sq, 1)
                if has(i, b - 1):
                    wait(act, pe_r, i, b - 1)
                    wait(act, d_on, i, b - 2)
                    nc.scalar.activation(rb[:], bank(b, "R"), ACT.Copy).then_inc(a_r, 1)

                def exps(h):
                    wait(act, d_max, i, b, 4, h + 1)
                    nc.scalar.activation(ps[:, h, :], ps[:, h, :], ACT.Exp, bias=negmax[:, b % 2, h:h + 1], scale=-1.0,
                                         accum_out=rowsum[:, b % 2, h:h + 1]).then_inc(a_exp, 1)

                def probs(h):
                    wait(act, pe_t, i, b, 4, h + 1)
                    nc.scalar.activation(pt_hi[:, 0:CT, h, :], bank(b, f"T{h}").rearrange("p (t q) -> p t q", t=CT),
                                         ACT.Copy).then_inc(a_pt, 1)

                if has(i, b):
                    exps(0)
                    exps(1)
                    probs(0)
                if has(i, b - 1):
                    wait(act, d_on, i, b - 1)
                    wait(act, pe_y, i, b - 2)
                    nc.scalar.activation(o_hi[:], on[:], ACT.Copy).then_inc(a_o, 1)
                if has(i, b):
                    exps(2)
                    probs(1)
                if has(i, g2):
                    wait(act, pe_q, i, g2)
                    wait(act, d_u, i, g2 - 2)
                    nc.scalar.activation(raw[:, g2 % 2, 0:QW], bank(b, "Q"), ACT.Copy).then_inc(a_q, 1)
                if has(i, b):
                    exps(3)
                if b == B - 3 and has(i, B):
                    h1 = (i + B) // B if isinstance(i, int) else None
                    wait(act, pe_q, i, B - 1)
                    act.wait_ge(s_wraw, 16 * (h1 + 1) if h1 is not None else i * 2 + 32)
                    for k in range(KC):
                        split_w(i, b, k, k + 1, (0, QW)).then_inc(a_whi, 1)
                if has(i, g1):
                    wait(act, pe_qt, i, g1)
                    nc.scalar.activation(qt_hi[:], bank(b, "QT"), ACT.Copy).then_inc(a_qt, 1)
                    wait(act, pe_ktc, i, g1)
                    nc.scalar.activation(kt_hi[:, 0:L], bank(b, "KTC"), ACT.Copy).then_inc(a_ktc, 1)
                    wait(act, pe_ktn, i, g1)
                    nc.scalar.activation(kt_hi[:, L:KEYS], bank(b, "KTN")[:, 0:S], ACT.Copy).then_inc(a_ktn, 1)
                if has(i, b):
                    probs(2)
                if b == B - 2 and has(i, B):
                    wait(act, pe_kv, i, B - 1)
                    split_w(i, b, 0, KC, (QW, WW)).then_inc(a_whi, 1)
                if b == 0 and (not isinstance(i, int) or i > 0):
                    wait(act, pe_y, i, -1)
                    act.wait_ge(s_woraw, (i // B + 1) * 16 if isinstance(i, int) else i * 2 + 16)
                    for h in range(REP):
                        nc.scalar.activation(wo_hi[:, h * HID:(h + 1) * HID], wo_raw[:, h * HID:(h + 1) * HID], ACT.Copy).then_inc(a_wohi, 1)
                if has(i, b):
                    probs(3)
                    wait(act, pe_tn, i, b)
                    nc.scalar.activation(pt_hi[:, CT, :, :].rearrange("p h q -> p (h q)"), bank(b, "TN"), ACT.Copy).then_inc(a_pt, 1)

            def x_hi(half):
                src = wo_raw[:].rearrange("p (k n) -> p k n", k=KC)
                for c in range(B // 2):
                    b = half * (B // 2) + c
                    nc.scalar.activation(xt_hi[:, :, b * S:(b + 1) * S], src[:, :, c * S:(c + 1) * S], ACT.Copy).then_inc(a_xhi, 1)

            act.wait_ge(s_x0, 16)
            x_hi(0)
            act.wait_ge(s_wraw, 16)
            for k in range(KC):
                split_w(0, 0, k, k + 1, (0, QW)).then_inc(a_whi, 1)
            split_w(0, 0, 0, KC, (QW, WW)).then_inc(a_whi, 1)
            act.wait_ge(d_ang, 1)
            ang = ps[:, 0, 0:B * HALF].rearrange("p (b d) -> p b d", b=B)
            absang = ps[:, 1, 0:B * HALF].rearrange("p (b d) -> p b d", b=B)
            nc.scalar.activation(sin[:, :, 0:HALF], ang, ACT.Sin).then_inc(a_sincos, 1)
            nc.scalar.activation(cos[:], absang, ACT.Sin, bias=halfpi[:, 0:1], scale=-1.0).then_inc(a_sincos, 1)
            act.wait_ge(s_x1, 16)
            x_hi(1)
            act.wait_ge(s_woraw, 16)
            for h in range(REP):
                nc.scalar.activation(wo_hi[:, h * HID:(h + 1) * HID], wo_raw[:, h * HID:(h + 1) * HID], ACT.Copy).then_inc(a_wohi, 1)
            for b in range(-2, B):
                step(0, b)
            with act.Fori(B, G - B, B) as i:
                for b in range(B):
                    step(i, b)
            for b in range(B + 1):
                step(G - B, b)

            nW1 = KC * WL
            act.wait_ge(s_wraw, 16 * (HK + 1))
            act.wait_ge(pe_kv, G)
            nc.scalar.activation(w_hi[:, 0:nW1], w_raw[:, 0:nW1], ACT.Copy).then_inc(a_whi, 1)
            for b in range(B):
                act.wait_ge(pe_xt, b + 1)
                nc.scalar.activation(xt_hi[:, :, b * S:(b + 1) * S],
                                     ps_w[:, b % NBANK, :].rearrange("p (k s) -> p k s", k=KC), ACT.Copy).then_inc(a_xhi, 1)
                if b == 0:
                    act.wait_ge(s_woraw, 16 * (HK + 1))
                    act.wait_ge(pe_y, G)
                    nc.scalar.activation(wo_hi[:, 0:HID], wo_raw[:, 0:HID], ACT.Copy).then_inc(a_wohi, 1)
            for b in range(B):
                act.wait_ge(pe_ar, b + 1)
                act.wait_ge(d_lg, b + 1)
                nc.scalar.activation(hflat[:, b * ER:(b + 1) * ER], expert_bank(b)[:, 0:ER], ACT.Copy).then_inc(a_h, 1)
            act.wait_ge(d_gd, 1)
            nc.scalar.activation(ge[:], gd[:], ACT.Exp).then_inc(a_ge, 1)
            for c in range(2):
                act.wait_ge(pe_ht, c + 1)
                nc.scalar.activation(pt_hi[:, c, :, :].rearrange("p h q -> p (h q)"), ps_w[:, c, :], ACT.Copy).then_inc(a_ht, 1)

        @block.vector
        def _(dve):
            def low(out_ap, full, hi):
                return nc.vector.tensor_tensor(out_ap, full, hi.bitcast(F32), ALU.subtract)

            def step(i, b):
                g1 = b + 1

                def rowmax(h):
                    wait(dve, pe_s, i, b, 4, h + 1)
                    wait(dve, pe_tn, i, b - 1)
                    carry(dve, i, d_mark)
                    nc.vector.tensor_tensor_reduce(out=ps[:, h, :], in0=ps_s[:, h % 2, 0:KEYS], in1=mask[:, b % B, :],
                                                   scale=-SCALE, scalar=3.0e38, op0=ALU.add, op1=ALU.min,
                                                   accum_out=negmax[:, b % 2, h:h + 1]).then_inc(d_max, 1)

                def probs(h):
                    wait(dve, a_pt, i, b, 5, h + 1)
                    low(pt_lo[:, 0:CT, h, :], bank(b, f"T{h}").rearrange("p (t q) -> p t q", t=CT),
                        pt_hi[:, 0:CT, h, :]).then_inc(d_pt, 1)

                if has(i, b - 1):
                    wait(dve, a_exp, i, b - 1, 4)
                    wait(dve, pe_r, i, b - 2)
                    nc.vector.reciprocal(recip[:, (b - 1) % 2, :], rowsum[:, (b - 1) % 2, :]).then_inc(d_recip, 1)
                if has(i, b):
                    rowmax(0)
                if has(i, g1):
                    wait(dve, a_sq, i, g1)
                    wait(dve, p_rstd, i, g1 - 1)
                    nc.vector.tensor_reduce(sumsq[:], u[:], AX_X, ALU.add).then_inc(d_ss, 1)
                if has(i, b):
                    rowmax(1)
                    probs(0)
                if has(i, b - 1):
                    wait(dve, pe_o, i, b - 1)
                    wait(dve, a_r, i, b - 1)
                    wait(dve, a_o, i, b - 2)
                    wait(dve, d_olo, i, b - 2)
                    nc.vector.tensor_tensor(on[:], bank(b, "O"), rb[:], ALU.mult).then_inc(d_on, 1)
                if has(i, g1):
                    wait(dve, p_wr, i, g1)
                    wait(dve, d_ss, i, g1)
                    nc.vector.tensor_tensor(u[:].rearrange("p h d -> p (h d)"), raw[:, g1 % 2, 0:QW + D],
                                            wr[:].rearrange("p h d -> p (h d)"), ALU.mult).then_inc(d_u, 1)
                if has(i, b - 1):
                    wait(dve, a_o, i, b - 1)
                    low(o_lo[:], on[:], o_hi[:]).then_inc(d_olo, 1)
                if has(i, g1):
                    wait(dve, d_u, i, g1)
                    wait(dve, p_rot, i, g1 - 1, 2)
                    nc.vector.tensor_tensor(m2[:], u[:], sin[:, g1 % B, :].unsqueeze(1).to_broadcast([P, NH, D]),
                                            ALU.mult).then_inc(d_m2, 1)
                if has(i, b):
                    rowmax(2)
                    probs(1)
                    rowmax(3)
                if has(i, b - 1):
                    wait(dve, pe_y, i, b - 1)
                    yb = y[:, (b - 1) % B, :]
                    nc.vector.tensor_tensor(yb, bank(b, "Y"), yb, ALU.add).then_inc(d_y, 1)
                if b == B - 3 and has(i, B):
                    for k in range(KC):
                        dve.wait_ge(a_whi, (i // B + 1) * 5 + k + 1 if isinstance(i, int) else a5(i, k))
                        low(wl[:, k, 0:QW], wrw[:, k, 0:QW], wh[:, k, 0:QW]).then_inc(d_wlo, 1)
                if has(i, g1):
                    wait(dve, a_qt, i, g1)
                    low(qt_lo[:], bank(b, "QT"), qt_hi[:]).then_inc(d_qt, 1)
                    wait(dve, a_ktc, i, g1)
                    low(kt_lo[:, 0:L], bank(b, "KTC"), kt_hi[:, 0:L]).then_inc(d_ktc, 1)
                    wait(dve, a_ktn, i, g1)
                    low(kt_lo[:, L:KEYS], bank(b, "KTN")[:, 0:S], kt_hi[:, L:KEYS]).then_inc(d_ktn, 1)
                if has(i, b):
                    probs(2)
                if b == B - 2 and has(i, B):
                    dve.wait_ge(a_whi, (i // B + 2) * 5 if isinstance(i, int) else a5(i, 4))
                    low(wl[:, :, QW:WW], wrw[:, :, QW:WW], wh[:, :, QW:WW]).then_inc(d_wlo, 1)
                if b == 0 and (not isinstance(i, int) or i > 0):
                    for h in range(REP):
                        dve.wait_ge(a_wohi, i // B * 4 + h + 1 if isinstance(i, int) else (i >> 1) + (h + 1))
                        c = slice(h * HID, (h + 1) * HID)
                        low(wo_lo[:, c], wo_raw[:, c], wo_hi[:, c]).then_inc(d_wolo, 1)
                if has(i, b):
                    probs(3)
                    wait(dve, a_pt, i, b, 5)
                    low(pt_lo[:, CT, :, :].rearrange("p h q -> p (h q)"), bank(b, "TN"),
                        pt_hi[:, CT, :, :].rearrange("p h q -> p (h q)")).then_inc(d_pt, 1)

            def a5(i, k):
                return (i >> 3) * 5 + (5 + k + 1)

            n_tab = [0]

            def tab(ins):
                ins.then_inc(d_gate, 1)
                n_tab[0] += 1
                dve.wait_ge(d_gate, n_tab[0])

            dve.wait_ge(s_cst, 64)
            tab(nc.vector.tensor_copy(blkf[:].rearrange("p b t -> p (b t)"), cin[:, I_BLOCK:I_LEN]))
            tab(nc.vector.tensor_scalar(blkf[:], blkf[:], float(PSIZE), cst[:, C_SLOT:C_SLOT + 1], ALU.mult, ALU.add))
            nc.vector.tensor_scalar(rows[:], blkf[:], -float(PAGES * PSIZE), None, ALU.add).then_inc(d_rows, 1)
            def x_lo(half):
                src = wo_raw[:].rearrange("p (k n) -> p k n", k=KC)
                for c in range(B // 2):
                    b = half * (B // 2) + c
                    dve.wait_ge(a_xhi, b + 1)
                    low(xt_lo[:, :, b * S:(b + 1) * S], src[:, :, c * S:(c + 1) * S], xt_hi[:, :, b * S:(b + 1) * S]).then_inc(d_xlo, 1)

            x_lo(0)
            for k in range(KC):
                dve.wait_ge(a_whi, k + 1)
                low(wl[:, k, 0:QW], wrw[:, k, 0:QW], wh[:, k, 0:QW]).then_inc(d_wlo, 1)
            dve.wait_ge(a_whi, KC + 1)
            low(wl[:, :, QW:WW], wrw[:, :, QW:WW], wh[:, :, QW:WW]).then_inc(d_wlo, 1)
            tab(nc.vector.memset(halfpi[:], float(np.pi / 2)))
            tab(nc.vector.tensor_copy(lenf[:], cin[:, I_LEN:I_LANG]))
            tab(nc.vector.tensor_scalar(pos[:], lenf[:], cst[:, C_ROW:C_ROW + 1], None, ALU.add))
            ang = ps[:, 0, 0:B * HALF].rearrange("p (b d) -> p b d", b=B)
            absang = ps[:, 1, 0:B * HALF].rearrange("p (b d) -> p b d", b=B)
            turns = ps[:, 2, 0:B * HALF].rearrange("p (b d) -> p b d", b=B)
            whole = ps[:, 3, 0:B * HALF].bitcast(I32).rearrange("p (b d) -> p b d", b=B)
            tab(nc.vector.tensor_tensor(ang, cst[:, C_INVF:C_INVF + HALF].unsqueeze(1).to_broadcast([P, B, HALF]),
                                        pos[:].unsqueeze(2).to_broadcast([P, B, HALF]), ALU.mult))
            tab(nc.vector.tensor_scalar(whole, ang, float(1.0 / TWO_PI), None, ALU.mult))
            tab(nc.vector.tensor_copy(turns, whole))
            for part in (TWO_PI_A, TWO_PI_B, TWO_PI_C):
                tab(nc.vector.scalar_tensor_tensor(out=ang, in0=turns, scalar=-part, in1=ang, op0=ALU.mult, op1=ALU.add))
            tab(nc.vector.tensor_scalar(ang, ang, PI_BELOW, -PI_BELOW, ALU.min, ALU.max))
            nc.vector.scalar_tensor_tensor(out=absang, in0=ang, scalar=-1.0, in1=ang, op0=ALU.mult, op1=ALU.max).then_inc(d_ang, 1)
            for b in range(B):
                nc.vector.tensor_scalar(mask[:, b, :], rot[:].rearrange("p h d -> p (h d)"), lenf[:, b:b + 1], MASKED, ALU.is_ge,
                                        ALU.mult).then_inc(d_mask, 1)
            tab(nc.vector.tensor_copy(langf[:], cin[:, I_LANG:I_END]))
            for b in range(B):
                nc.vector.tensor_scalar(lang_bias[:, b, :], cst[:, C_EXPERT:C_ROW], langf[:, b:b + 1], LANG_BIAS,
                                        ALU.is_equal, ALU.mult).then_inc(d_mask, 1)
            dve.wait_ge(a_sincos, 2)
            nc.vector.tensor_scalar(sin[:, :, HALF:D], sin[:, :, 0:HALF], -1.0, None, ALU.mult).then_inc(d_tab, 1)
            x_lo(1)
            for h in range(REP):
                dve.wait_ge(a_wohi, h + 1)
                c = slice(h * HID, (h + 1) * HID)
                low(wo_lo[:, c], wo_raw[:, c], wo_hi[:, c]).then_inc(d_wolo, 1)
            dve.wait_ge(d_tab, 1)
            dve.wait_ge(d_mask, 2 * B)
            dve.wait_ge(s_y, 16)
            for b in range(-2, B):
                step(0, b)
            with dve.Fori(B, G - B, B) as i:
                for b in range(B):
                    step(i, b)
            for b in range(B + 1):
                step(G - B, b)

            nW1 = KC * WL
            dve.wait_ge(a_whi, 5 * HK + 1)
            low(w_lo[:, 0:nW1], w_raw[:, 0:nW1], w_hi[:, 0:nW1]).then_inc(d_wlo, 1)
            for b in range(B):
                dve.wait_ge(a_xhi, B + b + 1)
                low(xt_lo[:, :, b * S:(b + 1) * S], ps_w[:, b % NBANK, :].rearrange("p (k s) -> p k s", k=KC),
                    xt_hi[:, :, b * S:(b + 1) * S]).then_inc(d_xlo, 1)
                if b == 0:
                    dve.wait_ge(a_wohi, 4 * HK + 1)
                    low(wo_lo[:, 0:HID], wo_raw[:, 0:HID], wo_hi[:, 0:HID]).then_inc(d_wolo, 1)
            for b in range(B):
                dve.wait_ge(pe_ar, b + 1)
                nc.vector.tensor_tensor(logits[:, b, :], expert_bank(b)[:, ER:ER + E], lang_bias[:, b, :],
                                        ALU.add).then_inc(d_lg, 1)
            n_tab2 = n_tab[0]
            for b in range(B):
                dve.wait_ge(d_lg, b + 1)
                nc.vector.max(out=top[:, b, :], in_=logits[:, b, :]).then_inc(d_gate, 1)
            for b in range(B):
                dve.wait_ge(d_gate, n_tab2 + b + 1)
                nc.vector.max_index(out=topi[:, b, :], in_max=top[:, b, :], in_values=logits[:, b, :]).then_inc(d_gate, 1)
            n_tab[0] = n_tab2 + 2 * B
            dve.wait_ge(d_gate, n_tab[0])
            nc.vector.tensor_tensor(gd[:].unsqueeze(2), top[:, :, 1:2], top[:, :, 0:1], ALU.subtract).then_inc(d_gd, 1)
            tab(nc.vector.tensor_copy(topf[:], topi[:, :, 0:2]))
            dve.wait_ge(a_ge, 1)
            tab(nc.vector.tensor_scalar(gs[:], ge[:], 1.0, None, ALU.add))
            tab(nc.vector.reciprocal(gd[:], gs[:]))
            tab(nc.vector.tensor_scalar(gw[:, 0, :], gd[:], LORA_SCALING, None, ALU.mult))
            tab(nc.vector.tensor_tensor(gw[:, 1, :], gw[:, 0, :], ge[:], ALU.mult))
            for c in range(2):
                tab(nc.vector.tensor_tensor(gate[:, c, :, :], cst[:, C_EXPERT:C_ROW].unsqueeze(1).to_broadcast([P, B, E]),
                                            topf[:, :, c:c + 1].to_broadcast([P, B, E]), ALU.is_equal))
                tab(nc.vector.tensor_tensor(gate[:, c, :, :], gate[:, c, :, :], gw[:, c, :].unsqueeze(2).to_broadcast([P, B, E]), ALU.mult))
            tab(nc.vector.tensor_tensor(gate[:, 0, :, :], gate[:, 0, :, :], gate[:, 1, :, :], ALU.add))
            dve.wait_ge(a_h, B)
            hh = hflat[:, 0:B * ER].rearrange("p (e r) -> p e r", r=R)
            nc.vector.tensor_tensor(hh, hh, gate[:, 0, :, :].rearrange("p b e -> p (b e)").unsqueeze(2).to_broadcast([P, B * E, R]),
                                    ALU.mult).then_inc(d_hg, 1)
            for c in range(2):
                dve.wait_ge(a_ht, c + 1)
                low(pt_lo[:, c, :, :].rearrange("p h q -> p (h q)"), ps_w[:, c, :],
                    pt_hi[:, c, :, :].rearrange("p h q -> p (h q)")).then_inc(d_ht, 1)
            for b in range(B):
                dve.wait_ge(pe_out, b + 1)
                if b >= 2:
                    dve.wait_ge(s_out[b % 2], 16 * (b // 2))
                nc.vector.tensor_tensor((rb if b % 2 else on)[:], ps_w[:, 2 + b % 2, :], y[:, b, :], ALU.add).then_inc(d_fin, 1)

        @block.tensor
        def _(pe):
            def step(i, b):
                g1, g2 = b + 1, b + 2

                def scores(h):
                    if h == 0:
                        wait(pe, d_qt, i, b)
                        wait(pe, d_ktc, i, b)
                        wait(pe, d_ktn, i, b)
                    if h >= 2:
                        wait(pe, d_max, i, b, 4, h - 1)
                    else:
                        wait(pe, d_max, i, b - 1, 4, h + 3)
                    qh, ql = qt_hi[:, h * S:(h + 1) * S], qt_lo[:, h * S:(h + 1) * S]
                    for n, (a, c) in enumerate(((qh, kt_hi), (qh, kt_lo), (ql, kt_hi))):
                        nc.tensor.matmul(ps_s[:, h % 2, 0:L], a, c[:, 0:L], start=n == 0, stop=n == 2)
                        last = nc.tensor.matmul(ps_s[:, h % 2, L:KEYS], a, c[:, L:KEYS], start=n == 0, stop=n == 2)
                    last.then_inc(pe_s, 1)

                def turn_probs(h):
                    wait(pe, a_exp, i, b, 4, h + 1)
                    wait_bank(pe, i, b, f"T{h}")
                    for t in range(CT):
                        last = nc.tensor.transpose(bank(b, f"T{h}")[:, t * S:(t + 1) * S], ps[:, h, t * P:(t + 1) * P], ident)
                    last.then_inc(pe_t, 1)

                if has(i, b):
                    scores(0)
                    scores(1)
                if has(i, b - 1):
                    wait(pe, d_recip, i, b - 1)
                    wait_bank(pe, i, b, "R")
                    for h in range(REP):
                        last = nc.tensor.transpose(bank(b, "R")[:, h * S:(h + 1) * S],
                                                   recip[:, (b - 1) % 2, h:h + 1].to_broadcast([P, P]), ident)
                    last.then_inc(pe_r, 1)
                    wait(pe, d_pt, i, b - 1, 5)
                    wait(pe, p_v, i, b - 1, 2)
                    wait_bank(pe, i, b, "O")
                    three_passes(bank(b, "O"), [(v_hi[:, t, :], v_lo[:, t, :],
                                                 pt_hi[:, t, :, :].rearrange("p h q -> p (h q)"),
                                                 pt_lo[:, t, :, :].rearrange("p h q -> p (h q)")) for t in range(KT)]
                                 ).then_inc(pe_o, 1)
                if has(i, b):
                    turn_probs(0)
                    scores(2)
                if has(i, g2):
                    if isinstance(i, int) and i == 0:
                        pe.wait_ge(d_xlo, min(g2, B - 1) + 1)
                    if g2 % B == 0:
                        pe.wait_ge(d_wlo, ((i + g2) // B) * 5 + 4 if isinstance(i, int) else (i >> 3) * 5 + (g2 // B * 5 + 4))
                    wait_bank(pe, i, b, "Q")
                    tok = slice(g2 % B * S, (g2 % B + 1) * S)
                    three_passes(bank(b, "Q"), [(xt_hi[:, k, tok], xt_lo[:, k, tok], wh[:, k, 0:QW], wl[:, k, 0:QW])
                                                for k in range(KC)]).then_inc(pe_q, 1)
                if has(i, b):
                    turn_probs(1)
                    scores(3)
                if has(i, b - 1):
                    wait(pe, d_olo, i, b - 1)
                    if (b - 1) % B == 0:
                        pe.wait_ge(d_wolo, (i // B + 1) * 4 if isinstance(i, int) else (i >> 1) + 4)
                    wait_bank(pe, i, b, "Y")
                    three_passes(bank(b, "Y"), [(o_hi[:, h * S:(h + 1) * S], o_lo[:, h * S:(h + 1) * S],
                                                 wo_hi[:, h * HID:(h + 1) * HID], wo_lo[:, h * HID:(h + 1) * HID])
                                                for h in range(REP)]).then_inc(pe_y, 1)
                if has(i, g1):
                    wait(pe, p_rot, i, g1, 2)
                    wait_bank(pe, i, b, "QT")
                    for h in range(REP):
                        last = nc.tensor.transpose(bank(b, "QT")[:, h * S:(h + 1) * S], rot[:, h, :], ident)
                    last.then_inc(pe_qt, 1)
                    wait_kv(pe, i, g1)
                    wait_bank(pe, i, b, "KTC")
                    for t in range(CT):
                        last = nc.tensor.transpose(bank(b, "KTC")[:, t * P:(t + 1) * P], kv_raw[:, g1 % 2, t, 0:D], ident)
                    last.then_inc(pe_ktc, 1)
                    wait_bank(pe, i, b, "KTN")
                    nc.tensor.transpose(bank(b, "KTN")[:, 0:S], rot[:, REP, :], ident).then_inc(pe_ktn, 1)
                if has(i, b):
                    turn_probs(2)
                if has(i, g2):
                    if g2 % B == 0:
                        pe.wait_ge(d_wlo, ((i + g2) // B) * 5 + 5 if isinstance(i, int) else (i >> 3) * 5 + (g2 // B * 5 + 5))
                    wait_bank(pe, i, b, "KV")
                    tok = slice(g2 % B * S, (g2 % B + 1) * S)
                    three_passes(bank(b, "KV")[:, 0:2 * D], [(xt_hi[:, k, tok], xt_lo[:, k, tok], wh[:, k, QW:WW], wl[:, k, QW:WW])
                                                             for k in range(KC)]).then_inc(pe_kv, 1)
                if has(i, b):
                    turn_probs(3)
                    wait_bank(pe, i, b, "TN")
                    for h in range(REP):
                        last = nc.tensor.transpose(bank(b, "TN")[:, h * S:(h + 1) * S], ps[:, h, L:KEYS], ident)
                    last.then_inc(pe_tn, 1)

            pe.wait_ge(s_cst, 64)
            for b in range(-2, B):
                step(0, b)
            with pe.Fori(B, G - B, B) as i:
                for b in range(B):
                    step(i, b)
            for b in range(B + 1):
                step(G - B, b)

            w1h = w_hi[:, 0:KC * WL].rearrange("p (k n) -> p k n", k=KC)
            w1l = w_lo[:, 0:KC * WL].rearrange("p (k n) -> p k n", k=KC)
            pe.wait_ge(d_y, G)
            for b in range(B):
                if b >= NBANK:
                    pe.wait_ge(d_xlo, B + b - NBANK + 1)
                for k in range(KC):
                    last = nc.tensor.transpose(ps_w[:, b % NBANK, k * S:(k + 1) * S], y[:, b, k * P:(k + 1) * P], ident)
                last.then_inc(pe_xt, 1)
            pe.wait_ge(d_wlo, 5 * HK + 1)
            for b in range(B):
                pe.wait_ge(d_xlo, B + b + 1)
                if b >= NBANK:
                    pe.wait_ge(a_h, b - NBANK + 1)
                three_passes(expert_bank(b), [(xt_hi[:, k, b * S:(b + 1) * S], xt_lo[:, k, b * S:(b + 1) * S],
                                               w1h[:, k, HID:WL], w1l[:, k, HID:WL]) for k in range(KC)]).then_inc(pe_ar, 1)

            def base(b):
                if b >= 2:
                    pe.wait_ge(d_fin, b - 1)
                three_passes(ps_w[:, 2 + b % 2, :], [(xt_hi[:, k, b * S:(b + 1) * S], xt_lo[:, k, b * S:(b + 1) * S],
                                                      w1h[:, k, 0:HID], w1l[:, k, 0:HID]) for k in range(KC)], stop=False)

            def lora(b):
                pe.wait_ge(d_ht, b // NBANK + 1)
                c, j = b // 4, b % 4
                three_passes(ps_w[:, 2 + b % 2, :], [(pt_hi[:, c, j, :], pt_lo[:, c, j, :], wo_hi[:, 0:HID], wo_lo[:, 0:HID])],
                             start=False).then_inc(pe_out, 1)

            base(0)
            base(1)
            pe.wait_ge(d_hg, 1)
            for c in range(2):
                for j in range(4):
                    b = 4 * c + j
                    last = nc.tensor.transpose(ps_w[:, c, j * S:(j + 1) * S], hflat[:, b * ER:(b + 1) * ER], ident)
                last.then_inc(pe_ht, 1)
            pe.wait_ge(d_wolo, 4 * HK + 1)
            for b in range(B):
                if b >= 2:
                    base(b)
                lora(b)


def kernel(**inputs):
    import concourse.bacc as _bacc
    from concourse.bass_utils import run_bass_kernel_spmd as _run

    a = {k: np.asarray(v) for k, v in inputs.items()}
    rows = np.arange(P)

    def tiles(m):
        return m.reshape(KC, P, -1).transpose(1, 0, 2).reshape(P, -1)

    x = a["x"]
    xT = x.transpose(2, 0, 1).reshape(KC, P, 2, B * S // 2).transpose(2, 1, 0, 3).reshape(2, P, -1)
    q, k, v = (a["L0_cond_" + n].T for n in ("Wq", "Wk", "Wv"))
    wqkv = np.stack([tiles(np.concatenate([q[:, h * QW:(h + 1) * QW], k[:, h * D:(h + 1) * D], v[:, h * D:(h + 1) * D]], 1))
                     for h in range(HK)])
    wo = a["L0_cond_Wo"].T.reshape(HK, REP, D, HID).transpose(0, 2, 1, 3).reshape(HK, P, -1)
    kv = np.concatenate([a["L0_cond_k_cache"], a["L0_cond_v_cache"]], -1).transpose(2, 0, 1, 3).reshape(HK * PAGES * PSIZE, 2 * D)
    normw = np.broadcast_to(np.concatenate([a["L0_cond_q_norm_w"]] * REP + [a["L0_cond_k_norm_w"]]), (P, NH * D))
    w1 = tiles(np.concatenate([a["L1_cond_W"].T, a["L1_cond_A"].reshape(ER, HID).T, a["L1_cond_Wr"].T], 1))
    wB = a["L1_cond_B"].transpose(0, 2, 1).reshape(ER, HID)

    consts = np.zeros((P, C_END), np.float32)
    consts[:, C_INVF:C_IDENT] = np.float32(1) / (THETA ** (np.arange(0, D, 2) / D)).astype(np.float32)
    consts[:, C_IDENT:C_EXPERT] = np.eye(P)
    consts[:, C_EXPERT:C_ROW] = np.arange(E)
    consts[:, C_ROW] = rows
    consts[:, C_SLOT] = rows % PSIZE
    kpos = np.empty((P, KEYS), np.float32)
    kpos[:, 0:L] = np.arange(L)
    kpos[:, L:KEYS] = -2.0**32
    ints = np.empty((P, I_END), np.int32)
    pages = a["itok_Bx16_0_63"].reshape(B, CT, P // PSIZE)[:, :, rows // PSIZE]
    ints[:, I_BLOCK:I_LEN] = pages.transpose(2, 0, 1).reshape(P, B * CT)
    ints[:, I_LEN:I_LANG] = a["itok_B_207_1644"]
    ints[:, I_LANG:I_END] = a["itok_B_0_7"]

    arrays = {"xT": xT, "x": x, "wqkv": wqkv, "wo": wo, "kv": kv, "normw": normw, "kpos": kpos, "consts": consts, "ints": ints,
              "w1": w1, "wB": wB}
    arrays = {n: np.ascontiguousarray(m) for n, m in arrays.items()}
    nc = _bacc.Bacc("TRN2", target_bir_lowering=False, num_devices=1)
    args = {n: nc.dram_tensor(n, m.shape, mybir.dt.from_np(m.dtype), kind="ExternalInput").ap() for n, m in arrays.items()}
    out = nc.dram_tensor("out", (B, S, HID), F32, kind="ExternalOutput").ap()
    attention_lora(nc, *args.values(), out)
    r = _run(nc, [arrays], core_ids=[0])
    return r.results[0]["out"]
```

```python
from contextlib import ExitStack

import numpy as np
import concourse.bass as bass
from concourse import mybir

F32 = mybir.dt.float32
F32R = mybir.dt.float32r
BF16 = mybir.dt.bfloat16
I32 = mybir.dt.int32
U32 = mybir.dt.uint32
ALU = mybir.AluOpType
ACT = mybir.ActivationFunctionType
AX_X = mybir.AxisListType.X

P = 128
B = 8
S = 128
HID = 512
D = 128
HALF = D // 2
HK = 8
REP = 4
HQ = HK * REP
PAGES, PSIZE, NPP = 64, 32, 16
L = PSIZE * NPP
KEYS = L + S
KT = KEYS // P
CT = L // P
KC = HID // P
QW = REP * D
WW = QW + 2 * D
NH = REP + 1
G = HK * B
E, R = 8, 16
ER = E * R
WL = HID + ER + E
SCALE = 1.0 / float(np.sqrt(D))
NORM_EPS = 1e-6
MASKED = -1e30
LANG_BIAS = 5.0
LORA_SCALING = 32.0 / 16.0
THETA = 10000.0

C_INVF = 0
C_IDENT = C_INVF + HALF
C_EXPERT = C_IDENT + P
C_ROW = C_EXPERT + E
C_SLOT = C_ROW + 1
C_END = C_SLOT + 1
I_BLOCK = 0
I_LEN = I_BLOCK + B * CT
I_LANG = I_LEN + B
I_END = I_LANG + B

TWO_PI = 2.0 * np.pi
TWO_PI_A = 6.28125
TWO_PI_B = float(np.float32(int((TWO_PI - TWO_PI_A) * 2**20) / 2**20))
TWO_PI_C = float(np.float32(TWO_PI - TWO_PI_A - TWO_PI_B))
PI_BELOW = 3.1415925

UNITS = ["O", "T0", "Q", "T1", "Y", "T2", "QT", "KTC", "KV", "KTN", "T3", "TN"]
NU = len(UNITS)
NBANK = 4
TURN_X = {(6, "Q"): 0, (6, "KV"): 1, (7, "Q"): 2, (7, "QT"): 3, (7, "KTC"): 4, (7, "KTN"): 5, (7, "KV"): 6}


def attention_lora(nc, xT, x, wqkv, wo, kv, normw, kpos, consts, ints, w1, wB, out):
    with ExitStack() as ctx:
        def sb(name, shape, dt=F32):
            return ctx.enter_context(nc.sbuf_tensor(name, shape, dt))

        def sem(name):
            return ctx.enter_context(nc.semaphore(name))

        xt_hi, xt_lo = sb("xt_hi", [P, KC, B * S], F32R), sb("xt_lo", [P, KC, B * S], F32R)
        w_raw = sb("w_raw", [P, KC * WW])
        w_hi, w_lo = sb("w_hi", [P, KC * WW], F32R), sb("w_lo", [P, KC * WW], F32R)
        wo_raw = sb("wo_raw", [P, REP * HID])
        wo_hi, wo_lo = sb("wo_hi", [P, REP * HID], F32R), sb("wo_lo", [P, REP * HID], F32R)
        kv_raw = sb("kv_raw", [P, 2, CT, 2 * D])
        y = sb("y", [P, B, HID])
        mask = sb("mask", [P, B, KEYS], BF16)
        cos = sb("cos", [P, B, HALF])
        sin = sb("sin", [P, B, D])
        cst = sb("cst", [P, C_END])
        cin = sb("cin", [P, I_END], I32)
        nw = sb("nw", [P, NH, D])
        raw = sb("raw", [P, 2, WW])
        wr = sb("wr", [P, NH, D])
        u = sb("u", [P, NH, D])
        rot = sb("rot", [P, NH, D])
        m2 = sb("m2", [P, NH, D])
        qt_hi, qt_lo = sb("qt_hi", [P, QW], F32R), sb("qt_lo", [P, QW], F32R)
        kt_hi, kt_lo = sb("kt_hi", [P, KEYS], F32R), sb("kt_lo", [P, KEYS], F32R)
        v_hi, v_lo = sb("v_hi", [P, KT, D], F32R), sb("v_lo", [P, KT, D], F32R)
        ps = sb("ps", [P, REP, KEYS])
        pt_hi, pt_lo = sb("pt_hi", [P, KT, REP, S], F32R), sb("pt_lo", [P, KT, REP, S], F32R)
        res = sb("res", [P, 2, HID])
        o_hi, o_lo = sb("o_hi", [P, REP * S], F32R), sb("o_lo", [P, REP * S], F32R)
        negmax = sb("negmax", [P, 2, REP])
        rowsum = sb("rowsum", [P, 2, REP])
        recip = sb("recip", [P, 2, REP])
        sumsq = sb("sumsq", [P, NH])
        meansq = sb("meansq", [P, NH])
        rstd = sb("rstd", [P, NH])
        mhalf = sb("mhalf", [P, NH])
        pos = sb("pos", [P, B])
        lenf = sb("lenf", [P, B])
        langf = sb("langf", [P, B])
        halfpi = sb("halfpi", [P, 1])
        blkf = sb("blkf", [P, B, CT])
        rows = sb("rows", [P, B, CT], I32)
        lang_bias = sb("lang_bias", [P, B, E])
        logits = sb("logits", [P, B, E])
        top = sb("top", [P, B, 8])
        topi = sb("topi", [P, B, 8], U32)
        topf = sb("topf", [P, B, 2])
        gd = sb("gd", [P, B])
        ge = sb("ge", [P, B])
        gs = sb("gs", [P, B])
        gw = sb("gw", [P, 2, B])
        gate = sb("gate", [P, 2, B, E])

        ident = cst[:, C_IDENT:C_IDENT + P]
        wh = w_hi[:].rearrange("p (k n) -> p k n", k=KC)
        wl = w_lo[:].rearrange("p (k n) -> p k n", k=KC)
        wrw = w_raw[:].rearrange("p (k n) -> p k n", k=KC)
        ps_s = ctx.enter_context(nc.psum_tensor("ps_s", [P, 2, 1024], F32))
        ps_w = ctx.enter_context(nc.psum_tensor("ps_w", [P, NBANK, 512], F32))

        s_ints, s_cst, s_tables = sem("ints_landed"), sem("consts_landed"), sem("norms_and_key_numbers_landed")
        s_x0, s_x1, s_y, s_out = sem("x0_landed"), sem("x1_landed"), sem("y_landed"), [sem("out_stored0"), sem("out_stored1")]
        s_w0 = [sem(f"first_wqkv{k}_landed") for k in range(KC)]
        s_wraw, s_woraw = sem("wqkv_landed"), sem("wo_landed")
        s_kv = [sem("kv0_landed"), sem("kv1_landed")]
        pe_q, pe_kv, pe_qt, pe_ktc, pe_ktn = sem("pe_q"), sem("pe_kv"), sem("pe_qt"), sem("pe_ktc"), sem("pe_ktn")
        pe_s, pe_t, pe_tn, pe_o, pe_y = sem("pe_s"), sem("pe_t"), sem("pe_tn"), sem("pe_o"), sem("pe_y")
        pe_xt, pe_ar, pe_ht, pe_out = sem("pe_xt"), sem("pe_ar"), sem("pe_ht"), sem("pe_out")
        a_xhi, a_whi, a_wohi = sem("a_xhi"), sem("a_whi"), sem("a_wohi")
        a_sincos, a_exp, a_q, a_kv, a_sq = sem("a_sincos"), sem("a_exp"), sem("a_q"), sem("a_kv"), sem("a_sq")
        a_qt, a_ktc, a_ktn, a_pt, a_norm, a_o = sem("a_qt"), sem("a_ktc"), sem("a_ktn"), sem("a_pt"), sem("a_norm"), sem("a_o")
        a_h, a_ge, a_ht = sem("a_h"), sem("a_ge"), sem("a_ht")
        d_tab, d_xlo, d_wlo, d_wolo, d_rows = sem("d_tab"), sem("d_xlo"), sem("d_wlo"), sem("d_wolo"), sem("d_rows")
        d_mask, d_ang, d_ss, d_u, d_m2 = sem("d_mask"), sem("d_ang"), sem("d_ss"), sem("d_u"), sem("d_m2")
        d_qt, d_ktc, d_ktn, d_max, d_pt = sem("d_qt"), sem("d_ktc"), sem("d_ktn"), sem("d_max"), sem("d_pt")
        d_recip, d_olo, d_y = sem("d_recip"), sem("d_olo"), sem("d_y")
        d_gate, d_lg, d_gd, d_hg, d_ht, d_fin = sem("d_gate"), sem("d_lg"), sem("d_gd"), sem("d_hg"), sem("d_ht"), sem("d_fin")
        d_mark, p_mark = sem("d_mark"), sem("p_mark")
        p_init, p_ms, p_rstd, p_wr, p_m1, p_rot = sem("p_init"), sem("p_ms"), sem("p_rstd"), sem("p_wr"), sem("p_m1"), sem("p_rot")
        p_vhi, p_v, p_rows = sem("p_vhi"), sem("p_v"), sem("p_rows")

        def has(i, off):
            return not isinstance(i, int) or 0 <= i + off < G

        def wait(eng, s, i, off, per=1, nth=None):
            add = off * per + (per if nth is None else nth)
            if isinstance(i, int):
                if i + off >= 0:
                    eng.wait_ge(s, i * per + add)
            else:
                eng.wait_ge(s, (i if per == 1 else i * per) + add)

        def carry(eng, i, mark):
            if not isinstance(i, int):
                eng.sem_inc(mark, 1)

        def wait_kv(eng, i, off):
            eng.wait_ge(s_kv[off % 2], i * 32 + 64 * (off // 2 + 1))

        def bank(unit):
            return ps_w[:, UNITS.index(unit) % NBANK, :]

        FREES = {"O": (d_olo, 1, 1, -1), "T0": (d_pt, 5, 1, 0), "Q": (a_q, 1, 1, 2), "T1": (d_pt, 5, 2, 0),
                 "QT": (d_qt, 1, 1, 1), "KTC": (d_ktc, 1, 1, 1), "KTN": (d_ktn, 1, 1, 1), "Y": (d_y, 1, 1, -1),
                 "T2": (d_pt, 5, 3, 0), "KV": (a_kv, 1, 1, 2), "T3": (d_pt, 5, 4, 0), "TN": (d_pt, 5, 5, 0)}

        def turned(i, b, unit):
            return TURN_X.get((b, unit)) if isinstance(i, int) and i == G - B else None

        def wait_bank(pe, i, b, unit):
            n = UNITS.index(unit)
            while True:
                n -= NBANK
                if n < 0:
                    n, b = n + NU, b - 1
                if b < -2:
                    return
                s, per, nth, off = FREES[UNITS[n]]
                if turned(i, b, UNITS[n]) is not None:
                    pe.wait_ge(d_xlo, B + turned(i, b, UNITS[n]) + 1)
                    return
                if has(i, b + off):
                    wait(pe, s, i, b + off, per, nth)
                    return

        def next_split(i, k):
            return (i >> 3) * SPLITS + (SPLITS + k + 1)

        SPLITS = KC + 2
        LAST_TURN = 3

        def three_passes(out_ap, pairs, start=True, stop=True, before=None):
            n = len(pairs)
            last = None
            for k, (a_hi, a_lo, b_hi, b_lo) in enumerate(pairs):
                if before is not None:
                    before(k)
                nc.tensor.matmul(out_ap, a_hi, b_hi, start=start and k == 0, stop=False)
                nc.tensor.matmul(out_ap, a_hi, b_lo, start=False, stop=False)
                last = nc.tensor.matmul(out_ap, a_lo, b_hi, start=False, stop=stop and k == n - 1)
            return last


        def expert_bank(b):
            return ps_s[:, b % 2, b // 2 % 2 * 512:b // 2 % 2 * 512 + ER + E]

        def result_bank(b):
            n = b % 6
            return ps_w[:, 2 + n, :] if n < 2 else ps_s[:, n % 2, (n - 2) // 2 * 512:(n - 2) // 2 * 512 + 512]

        hflat = ps[:].rearrange("p h k -> p (h k)")

        block = ctx.enter_context(nc.Block())

        @block.sync
        def _(sp):
            sp.dma_start(cin[:], ints[:, :]).then_inc(s_ints, 16)
            sp.dma_start(cst[:], consts[:, :]).then_inc(s_cst, 16)
            sp.dma_start(y[:, 0:B // 2, :].rearrange("p b h -> p (b h)"), xT[0]).then_inc(s_x0, 16)
            for k in range(KC):
                sp.dma_start(wrw[:, k, :], wqkv[0].rearrange("p (k n) -> p k n", k=KC)[:, k, :]).then_inc(s_w0[k], 16)
            sp.dma_start(nw[:].rearrange("p h d -> p (h d)"), normw[:, :]).then_inc(s_tables, 16)
            sp.dma_start(rot[:].rearrange("p h d -> p (h d)"), kpos[:, :]).then_inc(s_tables, 16)
            sp.dma_start(y[:, B // 2:B, :].rearrange("p b h -> p (b h)"), xT[1]).then_inc(s_x1, 16)
            sp.dma_start(wo_raw[:], wo[0]).then_inc(s_woraw, 16)
            sp.wait_ge(d_xlo, B)
            sp.dma_start(y[:], x.rearrange("b s h -> s b h")).then_inc(s_y, 16)

            def next_weights(h):
                sp.wait_ge(d_wlo, h * SPLITS)
                sp.dma_start(w_raw[:], wqkv[h]).then_inc(s_wraw, 16)
                sp.wait_ge(d_wolo, h * 4)
                sp.dma_start(wo_raw[:], wo[h]).then_inc(s_woraw, 16)

            with sp.Fori(1, HK) as h:
                next_weights(h)
            sp.wait_ge(d_wlo, HK * SPLITS)
            sp.dma_start(w_raw[:, 0:KC * WL], w1[:, :]).then_inc(s_wraw, 16)
            sp.wait_ge(d_wolo, HK * 4)
            sp.dma_start(wo_raw[:, 0:HID], wB[:, :]).then_inc(s_woraw, 16)
            for b in range(B):
                sp.wait_ge(d_fin, b + 1)
                sp.dma_start(out[b], res[:, b % 2, :]).then_inc(s_out[b % 2], 16)
            for stored in s_out:
                sp.wait_ge(stored, 16 * B // 2)

        @block.gpsimd
        def _(pool):
            nc.gpsimd.memset(mhalf[:], -0.5).then_inc(p_init, 1)

            def gather(b):
                pool.wait_ge(d_rows, 1)
                nc.gpsimd.tensor_scalar(rows[:, b % B, :], rows[:, b % B, :], float(PAGES * PSIZE), None,
                                        ALU.add).then_inc(p_rows, 1)

            def gather_dma(i, b):
                wait(pool, p_rows, i, b)
                wait(pool, pe_ktc, i, b - 2)
                wait(pool, p_v, i, b - 2, 2)
                carry(pool, i, p_mark)
                for t in range(CT):
                    pool.indirect_dma_start(kv_raw[:, b % 2, t, :], None, kv[:, :],
                                            bass.IndirectOffsetOnAxis(rows[:, b % B, t:t + 1], 0)
                                            ).then_inc(s_kv[b % 2], 16)

            def step(i, b):
                g1 = b + 1
                if has(i, g1):
                    wait(pool, d_ss, i, g1)
                    carry(pool, i, p_mark)
                    nc.gpsimd.tensor_scalar(meansq[:], sumsq[:], 1.0 / D, NORM_EPS, ALU.mult, ALU.add).then_inc(p_ms, 1)
                    wait(pool, p_ms, i, g1)
                    nc.gpsimd.tensor_tensor(rstd[:], meansq[:], mhalf[:], ALU.pow).then_inc(p_rstd, 1)
                    wait(pool, p_rstd, i, g1)
                    wait(pool, d_u, i, g1 - 1)
                    nc.gpsimd.tensor_tensor(wr[:], nw[:], rstd[:].unsqueeze(2).to_broadcast([P, NH, D]),
                                            ALU.mult).then_inc(p_wr, 1)
                    wait(pool, d_u, i, g1)
                    wait(pool, pe_ktn, i, g1 - 1)
                    nc.gpsimd.tensor_tensor(rot[:].rearrange("p h (t d) -> p (h t) d", t=2),
                                            u[:].rearrange("p h (t d) -> p (h t) d", t=2),
                                            cos[:, g1 % B, :].unsqueeze(1).to_broadcast([P, 2 * NH, HALF]),
                                            ALU.mult).then_inc(p_m1, 1)
                    wait(pool, p_m1, i, g1)
                    wait(pool, d_m2, i, g1)
                    for a, c in ((0, HALF), (HALF, 0)):
                        nc.gpsimd.tensor_tensor(rot[:, :, a:a + HALF], rot[:, :, a:a + HALF],
                                                m2[:, :, c:c + HALF], ALU.add).then_inc(p_rot, 1)
                if has(i, b):
                    wait_kv(pool, i, b)
                    wait(pool, a_kv, i, b)
                    wait(pool, pe_o, i, b - 1)
                    carry(pool, i, p_mark)
                    cached, new = kv_raw[:, b % 2, :, D:2 * D], raw[:, b % 2, QW + D:WW]
                    nc.gpsimd.tensor_copy(v_hi[:, 0:CT, :], cached).then_inc(p_vhi, 1)
                    nc.gpsimd.tensor_copy(v_hi[:, CT, :], new).then_inc(p_vhi, 1)
                    wait(pool, p_vhi, i, b, 2)
                    nc.gpsimd.tensor_tensor(v_lo[:, 0:CT, :], cached, v_hi[:, 0:CT, :].bitcast(F32), ALU.subtract).then_inc(p_v, 1)
                    nc.gpsimd.tensor_tensor(v_lo[:, CT, :], new, v_hi[:, CT, :].bitcast(F32), ALU.subtract).then_inc(p_v, 1)
                    if has(i, b + 2):
                        gather(b + 2)
                        gather_dma(i, b + 2)

            pool.wait_ge(d_rows, 1)
            for b in range(2):
                gather(b)
            for b in range(2):
                gather_dma(0, b)
            pool.wait_ge(s_tables, 32)
            pool.wait_ge(a_sincos, 2)
            pool.wait_ge(d_tab, 1)
            pool.wait_ge(d_mask, B)
            pool.wait_ge(p_init, 1)
            for b in range(-2, B):
                step(0, b)
            with pool.Fori(B, G - B, B) as i:
                for b in range(B):
                    step(i, b)
            for b in range(B + 1):
                step(G - B, b)

        @block.scalar
        def _(act):
            def split_w(k0, k1, c0, c1):
                nc.scalar.activation(wh[:, k0:k1, c0:c1], wrw[:, k0:k1, c0:c1], ACT.Copy).then_inc(a_whi, 1)

            def split_wo(h):
                c = slice(h * HID, (h + 1) * HID)
                nc.scalar.activation(wo_hi[:, c], wo_raw[:, c], ACT.Copy).then_inc(a_wohi, 1)

            def split_x(b):
                half, c = b // (B // 2), b % (B // 2)
                src = y[:, half * (B // 2):(half + 1) * (B // 2), :].rearrange("p b h -> p (b h)").rearrange("p (k n) -> p k n", k=KC)
                nc.scalar.activation(xt_hi[:, :, b * S:(b + 1) * S], src[:, :, c * S:(c + 1) * S], ACT.Copy).then_inc(a_xhi, 1)

            def turn_x(i, b, unit):
                c = turned(i, b, unit)
                if c is not None:
                    act.wait_ge(pe_xt, c + 1)
                    nc.scalar.activation(xt_hi[:, :, c * S:(c + 1) * S], bank(unit).rearrange("p (k s) -> p k s", k=KC),
                                         ACT.Copy).then_inc(a_xhi, 1)

            def step(i, b):
                g1, g2 = b + 1, b + 2
                last_head = isinstance(i, int) and i == G - B

                def exps(h):
                    wait(act, d_max, i, b, 4, h + 1)
                    nc.scalar.activation(ps[:, h, :], ps[:, h, :], ACT.Exp, bias=negmax[:, b % 2, h:h + 1], scale=-1.0,
                                         accum_out=rowsum[:, b % 2, h:h + 1]).then_inc(a_exp, 1)

                def norm(h):
                    wait(act, d_recip, i, b, 4, h + 1)
                    nc.scalar.activation(ps[:, h, :], ps[:, h, :], ACT.Copy, scale=recip[:, b % 2, h:h + 1]).then_inc(a_norm, 1)

                def probs(h):
                    wait(act, pe_t, i, b, 4, h + 1)
                    nc.scalar.activation(pt_hi[:, 0:CT, h, :], bank(f"T{h}").rearrange("p (t q) -> p t q", t=CT),
                                         ACT.Copy).then_inc(a_pt, 1)

                def query_weights(k):
                    if has(i, B):
                        if k == 0:
                            wait(act, pe_q, i, B - 1)
                            act.wait_ge(s_wraw, i * 2 + 16)
                        split_w(k, k + 1, 0, QW)

                def output_weights(h):
                    if h == 0:
                        wait(act, pe_y, i, -1)
                        act.wait_ge(s_woraw, i * 2 + 16)
                    split_wo(h)

                if has(i, g1):
                    wait(act, pe_kv, i, g1)
                    wait(act, p_v, i, g1 - 2, 2)
                    nc.scalar.activation(raw[:, g1 % 2, QW:WW], bank("KV")[:, 0:2 * D], ACT.Copy).then_inc(a_kv, 1)
                    wait(act, a_kv, i, g1)
                    wait(act, a_q, i, g1)
                    wait(act, d_m2, i, g1 - 1)
                    wait(act, p_m1, i, g1 - 1)
                    nc.scalar.activation(u[:].rearrange("p h d -> p (h d)"), raw[:, g1 % 2, 0:QW + D], ACT.Square).then_inc(a_sq, 1)
                if b == 1:
                    output_weights(1)
                if b == B - 2:
                    query_weights(2)
                if has(i, b):
                    exps(0)
                    norm(0)
                    exps(1)
                    norm(1)
                if b == B - 2:
                    query_weights(3)
                if has(i, b - 1):
                    wait(act, pe_o, i, b - 1)
                    wait(act, pe_y, i, b - 2)
                    nc.scalar.activation(o_hi[:], bank("O"), ACT.Copy).then_inc(a_o, 1)
                if has(i, b):
                    probs(0)
                    exps(2)
                    norm(2)
                if b == 1:
                    output_weights(2)
                if has(i, g2):
                    wait(act, pe_q, i, g2)
                    wait(act, d_u, i, g2 - 2)
                    nc.scalar.activation(raw[:, g2 % 2, 0:QW], bank("Q"), ACT.Copy).then_inc(a_q, 1)
                turn_x(i, b, "Q")
                if b == 1:
                    output_weights(3)
                if b == B - 3:
                    query_weights(0)
                if b == B - 2 and has(i, B):
                    wait(act, pe_kv, i, B - 1)
                    split_w(0, KC // 2, QW, WW)
                if isinstance(i, int) and i == 0 and b <= 0:
                    for c in (b * 2 + 6, b * 2 + 7):
                        if c == B // 2:
                            act.wait_ge(s_x1, 16)
                        split_x(c)
                if has(i, b):
                    probs(1)
                    exps(3)
                    norm(3)
                if b == 0:
                    output_weights(0)
                if b == B - 3:
                    query_weights(1)
                if b == B - 2 and has(i, B):
                    split_w(KC // 2, KC, QW, WW)
                if b == B - 2 and last_head:
                    wait(act, pe_kv, i, B - 1)
                    act.wait_ge(s_wraw, 16 * HK)
                    for k in range(KC):
                        nc.scalar.activation(w_hi[:, k * WL:(k + 1) * WL], w_raw[:, k * WL:(k + 1) * WL], ACT.Copy).then_inc(a_whi, 1)
                if has(i, b):
                    probs(2)
                if has(i, g1):
                    wait(act, pe_qt, i, g1)
                    nc.scalar.activation(qt_hi[:], bank("QT"), ACT.Copy).then_inc(a_qt, 1)
                    wait(act, pe_ktc, i, g1)
                    nc.scalar.activation(kt_hi[:, 0:L], bank("KTC"), ACT.Copy).then_inc(a_ktc, 1)
                    wait(act, pe_ktn, i, g1)
                    nc.scalar.activation(kt_hi[:, L:KEYS], bank("KTN")[:, 0:S], ACT.Copy).then_inc(a_ktn, 1)
                for unit in ("QT", "KTC", "KV", "KTN"):
                    turn_x(i, b, unit)
                if has(i, b):
                    probs(3)
                    wait(act, pe_tn, i, b)
                    nc.scalar.activation(pt_hi[:, CT, :, :].rearrange("p h q -> p (h q)"), bank("TN"), ACT.Copy).then_inc(a_pt, 1)

            act.wait_ge(s_x0, 16)
            split_x(0)
            split_x(1)
            for k in range(KC):
                act.wait_ge(s_w0[k], 16)
                split_w(k, k + 1, 0, QW)
            split_w(0, KC // 2, QW, WW)
            split_w(KC // 2, KC, QW, WW)
            act.wait_ge(d_ang, 1)
            ang = ps[:, 0, 0:B * HALF].rearrange("p (b d) -> p b d", b=B)
            absang = ps[:, 1, 0:B * HALF].rearrange("p (b d) -> p b d", b=B)
            nc.scalar.activation(sin[:, :, 0:HALF], ang, ACT.Sin).then_inc(a_sincos, 1)
            nc.scalar.activation(cos[:], absang, ACT.Sin, bias=halfpi[:, 0:1], scale=-1.0).then_inc(a_sincos, 1)
            for b in range(-2, B):
                step(0, b)
            with act.Fori(B, G - B, B) as i:
                for b in range(B):
                    step(i, b)
            for b in range(B + 1):
                step(G - B, b)

            act.wait_ge(s_woraw, 16 * (HK + 1))
            act.wait_ge(pe_y, G)
            nc.scalar.activation(wo_hi[:, 0:HID], wo_raw[:, 0:HID], ACT.Copy).then_inc(a_wohi, 1)

            def expert_products(b):
                act.wait_ge(pe_ar, b + 1)
                act.wait_ge(d_lg, b + 1)
                nc.scalar.activation(hflat[:, b * ER:(b + 1) * ER], expert_bank(b)[:, 0:ER], ACT.Copy).then_inc(a_h, 1)

            for b in range(B - 1):
                expert_products(b)
                if b == LAST_TURN:
                    act.wait_ge(pe_xt, B)
                    nc.scalar.activation(xt_hi[:, :, (B - 1) * S:B * S], ps_w[:, 0, :].rearrange("p (k s) -> p k s", k=KC),
                                         ACT.Copy).then_inc(a_xhi, 1)
            expert_products(B - 1)
            act.wait_ge(d_gd, 1)
            nc.scalar.activation(ge[:], gd[:], ACT.Exp).then_inc(a_ge, 1)
            for c in range(2):
                act.wait_ge(pe_ht, c + 1)
                nc.scalar.activation(pt_hi[:, c, :, :].rearrange("p h q -> p (h q)"), ps_w[:, c, :], ACT.Copy).then_inc(a_ht, 1)

        @block.vector
        def _(dve):
            def low(out_ap, full, hi):
                return nc.vector.tensor_tensor(out_ap, full, hi.bitcast(F32), ALU.subtract)

            def split_w(k0, k1, c0, c1):
                low(wl[:, k0:k1, c0:c1], wrw[:, k0:k1, c0:c1], wh[:, k0:k1, c0:c1]).then_inc(d_wlo, 1)

            def split_wo(i, h):
                dve.wait_ge(a_wohi, (i >> 1) + (h + 1))
                c = slice(h * HID, (h + 1) * HID)
                low(wo_lo[:, c], wo_raw[:, c], wo_hi[:, c]).then_inc(d_wolo, 1)

            def split_x(b):
                half, c = b // (B // 2), b % (B // 2)
                src = y[:, half * (B // 2):(half + 1) * (B // 2), :].rearrange("p b h -> p (b h)").rearrange("p (k n) -> p k n", k=KC)
                dve.wait_ge(a_xhi, b + 1)
                low(xt_lo[:, :, b * S:(b + 1) * S], src[:, :, c * S:(c + 1) * S], xt_hi[:, :, b * S:(b + 1) * S]).then_inc(d_xlo, 1)

            def turn_x(i, b, unit):
                c = turned(i, b, unit)
                if c is not None:
                    dve.wait_ge(a_xhi, B + c + 1)
                    low(xt_lo[:, :, c * S:(c + 1) * S], bank(unit).rearrange("p (k s) -> p k s", k=KC),
                        xt_hi[:, :, c * S:(c + 1) * S]).then_inc(d_xlo, 1)

            def step(i, b):
                g1 = b + 1
                last_head = isinstance(i, int) and i == G - B

                def rowmax(h):
                    wait(dve, pe_s, i, b, 4, h + 1)
                    wait(dve, pe_tn, i, b - 1)
                    carry(dve, i, d_mark)
                    nc.vector.tensor_tensor_reduce(out=ps[:, h, :], in0=ps_s[:, h % 2, 0:KEYS], in1=mask[:, b % B, :],
                                                   scale=-SCALE, scalar=3.0e38, op0=ALU.add, op1=ALU.min,
                                                   accum_out=negmax[:, b % 2, h:h + 1]).then_inc(d_max, 1)

                def over_sum(h):
                    wait(dve, a_exp, i, b, 4, h + 1)
                    wait(dve, a_norm, i, b - 2, 4)
                    nc.vector.reciprocal(recip[:, b % 2, h:h + 1], rowsum[:, b % 2, h:h + 1]).then_inc(d_recip, 1)

                def probs(h):
                    wait(dve, a_pt, i, b, 5, h + 1)
                    low(pt_lo[:, 0:CT, h, :], bank(f"T{h}").rearrange("p (t q) -> p t q", t=CT),
                        pt_hi[:, 0:CT, h, :]).then_inc(d_pt, 1)

                def query_weights(k):
                    if has(i, B):
                        dve.wait_ge(a_whi, next_split(i, k))
                        split_w(k, k + 1, 0, QW)

                def key_value_weights(c):
                    if has(i, B):
                        dve.wait_ge(a_whi, next_split(i, KC + c))
                        split_w(c * KC // 2, (c + 1) * KC // 2, QW, WW)

                if has(i, b):
                    rowmax(0)
                    rowmax(1)
                    over_sum(0)
                if has(i, g1):
                    wait(dve, a_sq, i, g1)
                    wait(dve, p_rstd, i, g1 - 1)
                    nc.vector.tensor_reduce(sumsq[:], u[:], AX_X, ALU.add).then_inc(d_ss, 1)
                if b == 1:
                    split_wo(i, 1)
                if b == B - 2:
                    query_weights(2)
                if has(i, b):
                    over_sum(1)
                if b == B - 2:
                    query_weights(3)
                if has(i, b - 1):
                    wait(dve, a_o, i, b - 1)
                    low(o_lo[:], bank("O"), o_hi[:]).then_inc(d_olo, 1)
                if has(i, b):
                    rowmax(2)
                if has(i, g1):
                    wait(dve, p_wr, i, g1)
                    wait(dve, d_ss, i, g1)
                    nc.vector.tensor_tensor(u[:].rearrange("p h d -> p (h d)"), raw[:, g1 % 2, 0:QW + D],
                                            wr[:].rearrange("p h d -> p (h d)"), ALU.mult).then_inc(d_u, 1)
                if has(i, b):
                    over_sum(2)
                if has(i, g1):
                    wait(dve, d_u, i, g1)
                    wait(dve, p_rot, i, g1 - 1, 2)
                    nc.vector.tensor_tensor(m2[:], u[:], sin[:, g1 % B, :].unsqueeze(1).to_broadcast([P, NH, D]),
                                            ALU.mult).then_inc(d_m2, 1)
                if has(i, b):
                    probs(0)
                if b == 1:
                    split_wo(i, 2)
                if has(i, b):
                    rowmax(3)
                if b == 1:
                    split_wo(i, 3)
                if b == B - 3:
                    query_weights(0)
                if b == B - 2:
                    key_value_weights(0)
                turn_x(i, b, "Q")
                if isinstance(i, int) and i == 0 and b <= 0:
                    for c in (b * 2 + 6, b * 2 + 7):
                        split_x(c)
                if has(i, b):
                    probs(1)
                    over_sum(3)
                if has(i, b - 1):
                    wait(dve, pe_y, i, b - 1)
                    yb = y[:, (b - 1) % B, :]
                    nc.vector.tensor_tensor(yb, bank("Y"), yb, ALU.add).then_inc(d_y, 1)
                if b == 0:
                    split_wo(i, 0)
                if b == B - 3:
                    query_weights(1)
                if b == B - 2:
                    key_value_weights(1)
                if b == B - 2 and last_head:
                    for k in range(KC):
                        dve.wait_ge(a_whi, SPLITS * HK + k + 1)
                        c = slice(k * WL, (k + 1) * WL)
                        low(w_lo[:, c], w_raw[:, c], w_hi[:, c]).then_inc(d_wlo, 1)
                if has(i, b):
                    probs(2)
                if has(i, g1):
                    wait(dve, a_qt, i, g1)
                    low(qt_lo[:], bank("QT"), qt_hi[:]).then_inc(d_qt, 1)
                    wait(dve, a_ktc, i, g1)
                    low(kt_lo[:, 0:L], bank("KTC"), kt_hi[:, 0:L]).then_inc(d_ktc, 1)
                    wait(dve, a_ktn, i, g1)
                    low(kt_lo[:, L:KEYS], bank("KTN")[:, 0:S], kt_hi[:, L:KEYS]).then_inc(d_ktn, 1)
                for unit in ("QT", "KTC", "KV", "KTN"):
                    turn_x(i, b, unit)
                if has(i, b):
                    probs(3)
                    wait(dve, a_pt, i, b, 5)
                    low(pt_lo[:, CT, :, :].rearrange("p h q -> p (h q)"), bank("TN"),
                        pt_hi[:, CT, :, :].rearrange("p h q -> p (h q)")).then_inc(d_pt, 1)

            n_tab = [0]

            def tab(ins):
                ins.then_inc(d_gate, 1)
                n_tab[0] += 1
                dve.wait_ge(d_gate, n_tab[0])

            dve.wait_ge(s_ints, 16)
            tab(nc.vector.tensor_copy(blkf[:].rearrange("p b t -> p (b t)"), cin[:, I_BLOCK:I_LEN]))
            dve.wait_ge(s_cst, 16)
            tab(nc.vector.tensor_scalar(blkf[:], blkf[:], float(PSIZE), cst[:, C_SLOT:C_SLOT + 1], ALU.mult, ALU.add))
            nc.vector.tensor_scalar(rows[:], blkf[:], -float(PAGES * PSIZE), None, ALU.add).then_inc(d_rows, 1)
            tab(nc.vector.memset(halfpi[:], float(np.pi / 2)))
            tab(nc.vector.tensor_copy(lenf[:], cin[:, I_LEN:I_LANG]))
            tab(nc.vector.tensor_scalar(pos[:], lenf[:], cst[:, C_ROW:C_ROW + 1], None, ALU.add))
            ang = ps[:, 0, 0:B * HALF].rearrange("p (b d) -> p b d", b=B)
            absang = ps[:, 1, 0:B * HALF].rearrange("p (b d) -> p b d", b=B)
            turns = ps[:, 2, 0:B * HALF].rearrange("p (b d) -> p b d", b=B)
            whole = ps[:, 3, 0:B * HALF].bitcast(I32).rearrange("p (b d) -> p b d", b=B)
            tab(nc.vector.tensor_tensor(ang, cst[:, C_INVF:C_INVF + HALF].unsqueeze(1).to_broadcast([P, B, HALF]),
                                        pos[:].unsqueeze(2).to_broadcast([P, B, HALF]), ALU.mult))
            tab(nc.vector.tensor_scalar(whole, ang, float(1.0 / TWO_PI), None, ALU.mult))
            tab(nc.vector.tensor_copy(turns, whole))
            for part in (TWO_PI_A, TWO_PI_B, TWO_PI_C):
                tab(nc.vector.scalar_tensor_tensor(out=ang, in0=turns, scalar=-part, in1=ang, op0=ALU.mult, op1=ALU.add))
            tab(nc.vector.tensor_scalar(ang, ang, PI_BELOW, -PI_BELOW, ALU.min, ALU.max))
            nc.vector.scalar_tensor_tensor(out=absang, in0=ang, scalar=-1.0, in1=ang, op0=ALU.mult, op1=ALU.max).then_inc(d_ang, 1)
            split_x(0)
            split_x(1)
            for k in range(KC):
                dve.wait_ge(a_whi, k + 1)
                split_w(k, k + 1, 0, QW)
            for c in range(2):
                dve.wait_ge(a_whi, KC + c + 1)
                split_w(c * KC // 2, (c + 1) * KC // 2, QW, WW)
            dve.wait_ge(a_sincos, 2)
            nc.vector.tensor_scalar(sin[:, :, HALF:D], sin[:, :, 0:HALF], -1.0, None, ALU.mult).then_inc(d_tab, 1)
            dve.wait_ge(s_tables, 32)
            for b in range(B):
                nc.vector.tensor_scalar(mask[:, b, :], rot[:].rearrange("p h d -> p (h d)"), lenf[:, b:b + 1], MASKED, ALU.is_ge,
                                        ALU.mult).then_inc(d_mask, 1)
            tab(nc.vector.tensor_copy(langf[:], cin[:, I_LANG:I_END]))
            dve.wait_ge(d_tab, 1)
            dve.wait_ge(d_mask, B)
            for b in range(-2, B):
                if b == 1:
                    dve.wait_ge(s_y, 16)
                step(0, b)
            with dve.Fori(B, G - B, B) as i:
                for b in range(B):
                    step(i, b)
            for b in range(B + 1):
                step(G - B, b)

            for b in range(B):
                nc.vector.tensor_scalar(lang_bias[:, b, :], cst[:, C_EXPERT:C_ROW], langf[:, b:b + 1], LANG_BIAS,
                                        ALU.is_equal, ALU.mult).then_inc(d_mask, 1)
            dve.wait_ge(d_mask, 2 * B)
            dve.wait_ge(a_wohi, 4 * HK + 1)
            low(wo_lo[:, 0:HID], wo_raw[:, 0:HID], wo_hi[:, 0:HID]).then_inc(d_wolo, 1)

            def biased(b):
                dve.wait_ge(pe_ar, b + 1)
                nc.vector.tensor_tensor(logits[:, b, :], expert_bank(b)[:, ER:ER + E], lang_bias[:, b, :],
                                        ALU.add).then_inc(d_lg, 1)

            for b in range(B - 1):
                biased(b)
                if b == LAST_TURN:
                    dve.wait_ge(a_xhi, 2 * B)
                    low(xt_lo[:, :, (B - 1) * S:B * S], ps_w[:, 0, :].rearrange("p (k s) -> p k s", k=KC),
                        xt_hi[:, :, (B - 1) * S:B * S]).then_inc(d_xlo, 1)
            biased(B - 1)
            n_tab2 = n_tab[0]
            for b in range(B):
                dve.wait_ge(d_lg, b + 1)
                nc.vector.max(out=top[:, b, :], in_=logits[:, b, :]).then_inc(d_gate, 1)
            for b in range(B):
                dve.wait_ge(d_gate, n_tab2 + b + 1)
                nc.vector.max_index(out=topi[:, b, :], in_max=top[:, b, :], in_values=logits[:, b, :]).then_inc(d_gate, 1)
            n_tab[0] = n_tab2 + 2 * B
            dve.wait_ge(d_gate, n_tab[0])
            nc.vector.tensor_tensor(gd[:].unsqueeze(2), top[:, :, 1:2], top[:, :, 0:1], ALU.subtract).then_inc(d_gd, 1)
            tab(nc.vector.tensor_copy(topf[:], topi[:, :, 0:2]))
            dve.wait_ge(a_ge, 1)
            tab(nc.vector.tensor_scalar(gs[:], ge[:], 1.0, None, ALU.add))
            tab(nc.vector.reciprocal(gd[:], gs[:]))
            tab(nc.vector.tensor_scalar(gw[:, 0, :], gd[:], LORA_SCALING, None, ALU.mult))
            tab(nc.vector.tensor_tensor(gw[:, 1, :], gw[:, 0, :], ge[:], ALU.mult))
            for c in range(2):
                tab(nc.vector.tensor_tensor(gate[:, c, :, :], cst[:, C_EXPERT:C_ROW].unsqueeze(1).to_broadcast([P, B, E]),
                                            topf[:, :, c:c + 1].to_broadcast([P, B, E]), ALU.is_equal))
                tab(nc.vector.tensor_tensor(gate[:, c, :, :], gate[:, c, :, :], gw[:, c, :].unsqueeze(2).to_broadcast([P, B, E]), ALU.mult))
            tab(nc.vector.tensor_tensor(gate[:, 0, :, :], gate[:, 0, :, :], gate[:, 1, :, :], ALU.add))
            dve.wait_ge(a_h, B)
            hh = hflat[:, 0:B * ER].rearrange("p (e r) -> p e r", r=R)
            nc.vector.tensor_tensor(hh, hh, gate[:, 0, :, :].rearrange("p b e -> p (b e)").unsqueeze(2).to_broadcast([P, B * E, R]),
                                    ALU.mult).then_inc(d_hg, 1)
            for c in range(2):
                dve.wait_ge(a_ht, c + 1)
                low(pt_lo[:, c, :, :].rearrange("p h q -> p (h q)"), ps_w[:, c, :],
                    pt_hi[:, c, :, :].rearrange("p h q -> p (h q)")).then_inc(d_ht, 1)
            for b in range(B):
                dve.wait_ge(pe_out, b + 1)
                if b >= 2:
                    dve.wait_ge(s_out[b % 2], 16 * (b // 2))
                nc.vector.tensor_tensor(res[:, b % 2, :], result_bank(b), y[:, b, :], ALU.add).then_inc(d_fin, 1)

        @block.tensor
        def _(pe):
            def turn_x(i, b, unit):
                c = turned(i, b, unit)
                if c is None:
                    return
                wait(pe, d_y, i, c)
                wait_bank(pe, i, b, unit)
                for k in range(KC):
                    last = nc.tensor.transpose(bank(unit)[:, k * S:(k + 1) * S], y[:, c, k * P:(k + 1) * P], ident)
                last.then_inc(pe_xt, 1)

            def step(i, b):
                g1, g2 = b + 1, b + 2
                tok = slice(g2 % B * S, (g2 % B + 1) * S)

                def scores(h):
                    if h == 0:
                        wait(pe, d_qt, i, b)
                        wait(pe, d_ktc, i, b)
                        wait(pe, d_ktn, i, b)
                    if h >= 2:
                        wait(pe, d_max, i, b, 4, h - 1)
                    else:
                        wait(pe, d_max, i, b - 1, 4, h + 3)
                    qh, ql = qt_hi[:, h * S:(h + 1) * S], qt_lo[:, h * S:(h + 1) * S]
                    for n, (a, c) in enumerate(((qh, kt_hi), (qh, kt_lo), (ql, kt_hi))):
                        nc.tensor.matmul(ps_s[:, h % 2, 0:L], a, c[:, 0:L], start=n == 0, stop=n == 2)
                        last = nc.tensor.matmul(ps_s[:, h % 2, L:KEYS], a, c[:, L:KEYS], start=n == 0, stop=n == 2)
                    last.then_inc(pe_s, 1)

                def turn_probs(h):
                    wait(pe, a_norm, i, b, 4, h + 1)
                    wait_bank(pe, i, b, f"T{h}")
                    for t in range(CT):
                        last = nc.tensor.transpose(bank(f"T{h}")[:, t * S:(t + 1) * S], ps[:, h, t * P:(t + 1) * P], ident)
                    last.then_inc(pe_t, 1)

                if has(i, b):
                    scores(0)
                    scores(1)
                if has(i, b - 1):
                    wait(pe, d_pt, i, b - 1, 5)
                    wait(pe, p_v, i, b - 1, 2)
                    wait_bank(pe, i, b, "O")
                    three_passes(bank("O"), [(v_hi[:, t, :], v_lo[:, t, :],
                                              pt_hi[:, t, :, :].rearrange("p h q -> p (h q)"),
                                              pt_lo[:, t, :, :].rearrange("p h q -> p (h q)")) for t in range(KT)]
                                 ).then_inc(pe_o, 1)
                if has(i, b):
                    scores(2)
                    turn_probs(0)
                if has(i, g2):
                    if isinstance(i, int) and i == 0:
                        pe.wait_ge(d_xlo, min(g2, B - 1) + 1)
                    wait_bank(pe, i, b, "Q")

                    def weights_split(k):
                        if b == -2:
                            pe.wait_ge(d_wlo, k + 1)
                        if g2 == B:
                            pe.wait_ge(d_wlo, next_split(i, k))

                    three_passes(bank("Q"), [(xt_hi[:, k, tok], xt_lo[:, k, tok], wh[:, k, 0:QW], wl[:, k, 0:QW])
                                             for k in range(KC)], before=weights_split).then_inc(pe_q, 1)
                turn_x(i, b, "Q")
                if has(i, b):
                    scores(3)
                    turn_probs(1)
                if has(i, b - 1):
                    wait(pe, d_olo, i, b - 1)
                    wait_bank(pe, i, b, "Y")

                    def output_weights_split(h):
                        if (b - 1) % B == 0:
                            pe.wait_ge(d_wolo, (i >> 1) + (h + 1))

                    three_passes(bank("Y"), [(o_hi[:, h * S:(h + 1) * S], o_lo[:, h * S:(h + 1) * S],
                                              wo_hi[:, h * HID:(h + 1) * HID], wo_lo[:, h * HID:(h + 1) * HID])
                                             for h in range(REP)], before=output_weights_split).then_inc(pe_y, 1)
                if has(i, b):
                    turn_probs(2)
                if has(i, g1):
                    wait(pe, p_rot, i, g1, 2)
                    wait_bank(pe, i, b, "QT")
                    for h in range(REP):
                        last = nc.tensor.transpose(bank("QT")[:, h * S:(h + 1) * S], rot[:, h, :], ident)
                    last.then_inc(pe_qt, 1)
                    wait_kv(pe, i, g1)
                    wait_bank(pe, i, b, "KTC")
                    for t in range(CT):
                        last = nc.tensor.transpose(bank("KTC")[:, t * P:(t + 1) * P], kv_raw[:, g1 % 2, t, 0:D], ident)
                    last.then_inc(pe_ktc, 1)
                turn_x(i, b, "QT")
                turn_x(i, b, "KTC")
                if has(i, g2):
                    if b == -2:
                        pe.wait_ge(d_wlo, SPLITS)
                    if g2 == B:
                        pe.wait_ge(d_wlo, next_split(i, SPLITS - 1))
                    wait_bank(pe, i, b, "KV")
                    three_passes(bank("KV")[:, 0:2 * D], [(xt_hi[:, k, tok], xt_lo[:, k, tok], wh[:, k, QW:WW], wl[:, k, QW:WW])
                                                          for k in range(KC)]).then_inc(pe_kv, 1)
                turn_x(i, b, "KV")
                if has(i, g1):
                    wait_bank(pe, i, b, "KTN")
                    nc.tensor.transpose(bank("KTN")[:, 0:S], rot[:, REP, :], ident).then_inc(pe_ktn, 1)
                turn_x(i, b, "KTN")
                if has(i, b):
                    turn_probs(3)
                    wait_bank(pe, i, b, "TN")
                    for h in range(REP):
                        last = nc.tensor.transpose(bank("TN")[:, h * S:(h + 1) * S], ps[:, h, L:KEYS], ident)
                    last.then_inc(pe_tn, 1)

            for b in range(-2, B):
                if b == -1:
                    pe.wait_ge(s_cst, 16)
                step(0, b)
            with pe.Fori(B, G - B, B) as i:
                for b in range(B):
                    step(i, b)
            for b in range(B + 1):
                step(G - B, b)

            w1h = w_hi[:, 0:KC * WL].rearrange("p (k n) -> p k n", k=KC)
            w1l = w_lo[:, 0:KC * WL].rearrange("p (k n) -> p k n", k=KC)

            def x_tiles(b, c0, c1):
                return [(xt_hi[:, k, b * S:(b + 1) * S], xt_lo[:, k, b * S:(b + 1) * S], w1h[:, k, c0:c1], w1l[:, k, c0:c1])
                        for k in range(KC)]

            def expert_products(b):
                pe.wait_ge(d_xlo, B + b + 1)
                if b >= NBANK:
                    pe.wait_ge(a_h, b - NBANK + 1)
                three_passes(expert_bank(b), x_tiles(b, HID, WL)).then_inc(pe_ar, 1)

            def base(b):
                if b >= 6:
                    pe.wait_ge(d_fin, b - 6 + 1)
                three_passes(result_bank(b), x_tiles(b, 0, HID), stop=False)

            def lora(b):
                pe.wait_ge(d_ht, b // NBANK + 1)
                c, j = b // 4, b % 4
                three_passes(result_bank(b), [(pt_hi[:, c, j, :], pt_lo[:, c, j, :], wo_hi[:, 0:HID], wo_lo[:, 0:HID])],
                             start=False).then_inc(pe_out, 1)

            pe.wait_ge(d_wlo, SPLITS * HK + KC)
            pe.wait_ge(d_max, 4 * G)
            for b in range(LAST_TURN + 1):
                expert_products(b)
            pe.wait_ge(d_y, G)
            for k in range(KC):
                last = nc.tensor.transpose(ps_w[:, 0, k * S:(k + 1) * S], y[:, B - 1, k * P:(k + 1) * P], ident)
            last.then_inc(pe_xt, 1)
            for b in range(LAST_TURN + 1, B - 1):
                expert_products(b)
            base(0)
            expert_products(B - 1)
            base(1)
            pe.wait_ge(a_h, B)
            for b in range(2, 6):
                base(b)
            pe.wait_ge(d_hg, 1)
            for c in range(2):
                for j in range(4):
                    b = 4 * c + j
                    last = nc.tensor.transpose(ps_w[:, c, j * S:(j + 1) * S], hflat[:, b * ER:(b + 1) * ER], ident)
                last.then_inc(pe_ht, 1)
            pe.wait_ge(d_wolo, 4 * HK + 1)
            for b in range(B):
                if b >= 6:
                    base(b)
                lora(b)


def kernel(**inputs):
    import concourse.bacc as _bacc
    from concourse.bass_utils import run_bass_kernel_spmd as _run

    a = {k: np.asarray(v) for k, v in inputs.items()}
    rows = np.arange(P)

    def tiles(m):
        return m.reshape(KC, P, -1).transpose(1, 0, 2).reshape(P, -1)

    x = a["x"]
    xT = x.transpose(2, 0, 1).reshape(KC, P, 2, B * S // 2).transpose(2, 1, 0, 3).reshape(2, P, -1)
    q, k, v = (a["L0_cond_" + n].T for n in ("Wq", "Wk", "Wv"))
    wqkv = np.stack([tiles(np.concatenate([q[:, h * QW:(h + 1) * QW], k[:, h * D:(h + 1) * D], v[:, h * D:(h + 1) * D]], 1))
                     for h in range(HK)])
    wo = a["L0_cond_Wo"].T.reshape(HK, REP, D, HID).transpose(0, 2, 1, 3).reshape(HK, P, -1)
    kv = np.concatenate([a["L0_cond_k_cache"], a["L0_cond_v_cache"]], -1).transpose(2, 0, 1, 3).reshape(HK * PAGES * PSIZE, 2 * D)
    normw = np.broadcast_to(np.concatenate([a["L0_cond_q_norm_w"]] * REP + [a["L0_cond_k_norm_w"]]), (P, NH * D))
    w1 = tiles(np.concatenate([a["L1_cond_W"].T, a["L1_cond_A"].reshape(ER, HID).T, a["L1_cond_Wr"].T], 1))
    wB = a["L1_cond_B"].transpose(0, 2, 1).reshape(ER, HID)

    consts = np.zeros((P, C_END), np.float32)
    consts[:, C_INVF:C_IDENT] = np.float32(1) / (THETA ** (np.arange(0, D, 2) / D)).astype(np.float32)
    consts[:, C_IDENT:C_EXPERT] = np.eye(P)
    consts[:, C_EXPERT:C_ROW] = np.arange(E)
    consts[:, C_ROW] = rows
    consts[:, C_SLOT] = rows % PSIZE
    kpos = np.empty((P, KEYS), np.float32)
    kpos[:, 0:L] = np.arange(L)
    kpos[:, L:KEYS] = -2.0**32
    ints = np.empty((P, I_END), np.int32)
    pages = a["itok_Bx16_0_63"].reshape(B, CT, P // PSIZE)[:, :, rows // PSIZE]
    ints[:, I_BLOCK:I_LEN] = pages.transpose(2, 0, 1).reshape(P, B * CT)
    ints[:, I_LEN:I_LANG] = a["itok_B_207_1644"]
    ints[:, I_LANG:I_END] = a["itok_B_0_7"]

    arrays = {"xT": xT, "x": x, "wqkv": wqkv, "wo": wo, "kv": kv, "normw": normw, "kpos": kpos, "consts": consts, "ints": ints,
              "w1": w1, "wB": wB}
    arrays = {n: np.ascontiguousarray(m) for n, m in arrays.items()}
    nc = _bacc.Bacc("TRN2", target_bir_lowering=False, num_devices=1)
    args = {n: nc.dram_tensor(n, m.shape, mybir.dt.from_np(m.dtype), kind="ExternalInput").ap() for n, m in arrays.items()}
    out = nc.dram_tensor("out", (B, S, HID), F32, kind="ExternalOutput").ap()
    attention_lora(nc, *args.values(), out)
    r = _run(nc, [arrays], core_ids=[0])
    return r.results[0]["out"]
```

```python
from contextlib import ExitStack

import numpy as np
import concourse.bass as bass
from concourse import mybir

F32 = mybir.dt.float32
F32R = mybir.dt.float32r
BF16 = mybir.dt.bfloat16
I32 = mybir.dt.int32
U32 = mybir.dt.uint32
ALU = mybir.AluOpType
ACT = mybir.ActivationFunctionType
AX_X = mybir.AxisListType.X

P = 128
B = 8
S = 128
HID = 512
D = 128
HALF = D // 2
HK = 8
REP = 4
PAGES, PSIZE, NPP = 64, 32, 16
L = PSIZE * NPP
KEYS = L + S
KT = KEYS // P
CT = L // P
KH = KEYS // 2
KC = HID // P
QW = REP * D
WW = QW + 2 * D
NH = REP + 1
G = HK * B
E, R = 8, 16
ER = E * R
WL = HID + ER + E
WLH = WL // 2
HB = B // 2
SCALE = 1.0 / float(np.sqrt(D))
NORM_EPS = 1e-6
MASKED = -1e30
LANG_BIAS = 5.0
LORA_SCALING = 32.0 / 16.0
THETA = 10000.0

C_INVF = 0
C_IDENT = C_INVF + HALF
C_EXPERT = C_IDENT + P
C_ROW = C_EXPERT + E
C_SLOT = C_ROW + 1
C_END = C_SLOT + 1
I_BLOCK = 0
I_LEN = I_BLOCK + B * CT
I_LANG = I_LEN + B
I_END = I_LANG + B

TWO_PI = 2.0 * np.pi
TWO_PI_A = 6.28125
TWO_PI_B = float(np.float32(int((TWO_PI - TWO_PI_A) * 2**20) / 2**20))
TWO_PI_C = float(np.float32(TWO_PI - TWO_PI_A - TWO_PI_B))
PI_BELOW = 3.1415925

UNITS = ["O", "T0", "Q", "T1", "Y", "T2", "QT", "KTC", "KV", "KTN", "T3", "TN"]
NU = len(UNITS)
NBANK = 4
TURN_X = {(6, "Q"): 0, (6, "KV"): 1, (7, "Q"): 2, (7, "QT"): 3, (7, "KTC"): 4, (7, "KTN"): 5, (7, "KV"): 6}


def attention_lora(nc, xT, x, wqkv, wo, kv, normw, kpos, consts, ints, w1, wB, out):
    with ExitStack() as ctx:
        def sb(name, shape, dt=F32):
            return ctx.enter_context(nc.sbuf_tensor(name, shape, dt))

        def sem(name):
            return ctx.enter_context(nc.semaphore(name))

        xt_hi, xt_lo = sb("xt_hi", [P, KC, B * S], F32R), sb("xt_lo", [P, KC, B * S], F32R)
        w_raw = sb("w_raw", [P, KC * WW])
        w_hi, w_lo = sb("w_hi", [P, KC * WW], F32R), sb("w_lo", [P, KC * WW], F32R)
        wo_raw = sb("wo_raw", [P, REP * HID])
        wo_hi, wo_lo = sb("wo_hi", [P, REP * HID], F32R), sb("wo_lo", [P, REP * HID], F32R)
        kv_raw = sb("kv_raw", [P, 2, CT, 2 * D])
        y = sb("y", [P, B, HID])
        mask = sb("mask", [P, B, KEYS], BF16)
        cos = sb("cos", [P, B, HALF])
        sin = sb("sin", [P, B, D])
        cst = sb("cst", [P, C_END])
        cin = sb("cin", [P, I_END], I32)
        nw = sb("nw", [P, NH, D])
        raw = sb("raw", [P, 2, WW])
        wr = sb("wr", [P, NH, D])
        u = sb("u", [P, NH, D])
        rot = sb("rot", [P, NH, D])
        m2 = sb("m2", [P, NH, D])
        qt_hi, qt_lo = sb("qt_hi", [P, QW], F32R), sb("qt_lo", [P, QW], F32R)
        kt_hi, kt_lo = sb("kt_hi", [P, KEYS], F32R), sb("kt_lo", [P, KEYS], F32R)
        v_hi, v_lo = sb("v_hi", [P, KT, D], F32R), sb("v_lo", [P, KT, D], F32R)
        ps = sb("ps", [P, REP, KEYS])
        pt_hi, pt_lo = sb("pt_hi", [P, KT, REP, S], F32R), sb("pt_lo", [P, KT, REP, S], F32R)
        o_hi, o_lo = sb("o_hi", [P, REP * S], F32R), sb("o_lo", [P, REP * S], F32R)
        negmax = sb("negmax", [P, 2, REP])
        rowsum = sb("rowsum", [P, 2, REP])
        recip = sb("recip", [P, 2, REP])
        sumsq = sb("sumsq", [P, NH])
        meansq = sb("meansq", [P, NH])
        rstd = sb("rstd", [P, NH])
        mhalf = sb("mhalf", [P, NH])
        pos = sb("pos", [P, B])
        lenf = sb("lenf", [P, B])
        langf = sb("langf", [P, B])
        halfpi = sb("halfpi", [P, 1])
        unused = sb("unused", [P, 1])
        blkf = sb("blkf", [P, B, CT])
        rows = sb("rows", [P, B, CT], I32)
        lang_bias = sb("lang_bias", [P, B, E])
        logits = sb("logits", [P, B, E])
        top = sb("top", [P, B, 16])
        topi = sb("topi", [P, 2, B, 8], U32)
        topf = sb("topf", [P, 2, B])
        others = sb("others", [P, B, E])
        gd = sb("gd", [P, B])
        ge = sb("ge", [P, B])
        gs = sb("gs", [P, B])
        gw = sb("gw", [P, 2, B])
        gate = sb("gate", [P, 2, B, E])

        ident = cst[:, C_IDENT:C_IDENT + P]
        wh = w_hi[:].rearrange("p (k n) -> p k n", k=KC)
        wl = w_lo[:].rearrange("p (k n) -> p k n", k=KC)
        wrw = w_raw[:].rearrange("p (k n) -> p k n", k=KC)
        ps_s = ctx.enter_context(nc.psum_tensor("ps_s", [P, 2, 2, 512], F32))
        ps_w = ctx.enter_context(nc.psum_tensor("ps_w", [P, NBANK, 512], F32))

        s_ints, s_cst, s_tables = sem("ints_landed"), sem("consts_landed"), sem("norms_and_key_numbers_landed")
        s_xt = [sem(f"x_transposed{n}_landed") for n in range(3)]
        s_y, s_out = [sem("x_first_half_landed"), sem("x_second_half_landed")], sem("out_stored")
        s_w0 = [sem(f"first_wqkv{k}_landed") for k in range(KC)]
        s_wraw, s_woraw = sem("wqkv_landed"), sem("wo_landed")
        s_kv = [sem("kv0_landed"), sem("kv1_landed")]
        pe_q, pe_kv, pe_qt, pe_ktc, pe_ktn = sem("pe_q"), sem("pe_kv"), sem("pe_qt"), sem("pe_ktc"), sem("pe_ktn")
        pe_s, pe_t, pe_tn, pe_o, pe_y = sem("pe_s"), sem("pe_t"), sem("pe_tn"), sem("pe_o"), sem("pe_y")
        pe_xt, pe_ar, pe_ht, pe_out = sem("pe_xt"), sem("pe_ar"), sem("pe_ht"), sem("pe_out")
        a_xhi, a_whi, a_wohi = sem("a_xhi"), sem("a_whi"), sem("a_wohi")
        a_sincos, a_exp, a_q, a_kv, a_sq = sem("a_sincos"), sem("a_exp"), sem("a_q"), sem("a_kv"), sem("a_sq")
        a_qt, a_ktc, a_ktn, a_pt, a_norm, a_o = sem("a_qt"), sem("a_ktc"), sem("a_ktn"), sem("a_pt"), sem("a_norm"), sem("a_o")
        a_vhi, a_table, a_h, a_ge, a_ht = sem("a_vhi"), sem("a_table"), sem("a_h"), sem("a_ge"), sem("a_ht")
        d_tab, d_xlo, d_wlo, d_wolo, d_rows = sem("d_tab"), sem("d_xlo"), sem("d_wlo"), sem("d_wolo"), sem("d_rows")
        d_mask, d_bias, d_ang, d_ss, d_u, d_m2 = sem("d_mask"), sem("d_bias"), sem("d_ang"), sem("d_ss"), sem("d_u"), sem("d_m2")
        d_qt, d_ktc, d_ktn, d_max, d_pt = sem("d_qt"), sem("d_ktc"), sem("d_ktn"), sem("d_max"), sem("d_pt")
        d_recip, d_olo, d_y = sem("d_recip"), sem("d_olo"), sem("d_y")
        d_base, d_gate, d_lg, d_gd, d_hg, d_ht, d_fin = sem("d_base"), sem("d_gate"), sem("d_lg"), sem("d_gd"), sem("d_hg"), sem("d_ht"), sem("d_fin")
        d_mark, p_mark = sem("d_mark"), sem("p_mark")
        p_init, p_ms, p_rstd, p_wr, p_m1, p_rot = sem("p_init"), sem("p_ms"), sem("p_rstd"), sem("p_wr"), sem("p_m1"), sem("p_rot")
        p_v, p_rows = sem("p_v"), sem("p_rows")


        def has(i, off):
            return not isinstance(i, int) or 0 <= i + off < G

        def wait(eng, s, i, off, per=1, nth=None):
            add = off * per + (per if nth is None else nth)
            if isinstance(i, int):
                if i + off >= 0:
                    eng.wait_ge(s, i * per + add)
            else:
                eng.wait_ge(s, (i if per == 1 else i * per) + add)

        def carry(eng, i, mark):
            if not isinstance(i, int):
                eng.sem_inc(mark, 1)

        def wait_kv(eng, i, off):
            eng.wait_ge(s_kv[off % 2], i * 32 + 64 * (off // 2 + 1))

        def bank(unit):
            return ps_w[:, UNITS.index(unit) % NBANK, :]

        FREES = {"O": (d_olo, 1, 1, -1), "T0": (d_pt, 5, 1, 0), "Q": (a_q, 1, 1, 2), "T1": (d_pt, 5, 2, 0),
                 "QT": (d_qt, 1, 1, 1), "KTC": (d_ktc, 1, 1, 1), "KTN": (d_ktn, 1, 1, 1), "Y": (d_y, 1, 1, -1),
                 "T2": (d_pt, 5, 3, 0), "KV": (a_kv, 1, 1, 2), "T3": (d_pt, 5, 4, 0), "TN": (d_pt, 5, 5, 0)}

        def first_keys(i, b):
            return isinstance(i, int) and i == 0 and b == -1

        def first_steps_x(i, b):
            if not (isinstance(i, int) and i == 0 and -1 <= b <= 3):
                return ()
            return (2, 3) if b < 0 else (b + 4,)

        def turned(i, b, unit):
            return TURN_X.get((b, unit)) if isinstance(i, int) and i == G - B else None

        def wait_bank(pe, i, b, unit):
            n = UNITS.index(unit)
            while True:
                n -= NBANK
                if n < 0:
                    n, b = n + NU, b - 1
                if b < -2:
                    return
                s, per, nth, off = FREES[UNITS[n]]
                if turned(i, b, UNITS[n]) is not None:
                    pe.wait_ge(d_xlo, B + turned(i, b, UNITS[n]) + 1)
                    return
                if has(i, b + off):
                    wait(pe, s, i, b + off, per, nth)
                    return

        def next_split(i, k):
            return (i >> 3) * SPLITS + (SPLITS + k + 1)

        SPLITS = KC + 2

        def three_passes(out_ap, pairs, start=True, stop=True, before=None):
            n = len(pairs)
            last = None
            for k, (a_hi, a_lo, b_hi, b_lo) in enumerate(pairs):
                if before is not None:
                    before(k)
                nc.tensor.matmul(out_ap, a_hi, b_hi, start=start and k == 0, stop=False)
                nc.tensor.matmul(out_ap, a_hi, b_lo, start=False, stop=False)
                last = nc.tensor.matmul(out_ap, a_lo, b_hi, start=False, stop=stop and k == n - 1)
            return last

        def last_step(i, b):
            return isinstance(i, int) and i == G - B and b == B

        def base_banks(b):
            return [(ps_s[:, b % 2, 1, 0:HID - WLH], slice(WLH, HID)), (ps_s[:, b % 2, 0, 0:WLH], slice(0, WLH))]

        def expert_bank(b):
            return ps_s[:, b % 2, 1, HID - WLH:WLH]

        def result_bank(b):
            if b == B - 1:
                return ps_s[:, 1, 0, :]
            return ps_w[:, 2 + b % 2, :] if b % 4 < 2 else ps_s[:, 0, b % 2, :]

        kpos_stage = raw[:, 1, 0:KEYS]

        def xt_stage(half, c0, c1):
            return y[:, half * HB:(half + 1) * HB, :].rearrange("p b h -> p (b h)").rearrange(
                "p (k n) -> p k n", k=KC)[:, :, c0 * S:c1 * S]

        hflat = ps[:].rearrange("p h k -> p (h k)")

        block = ctx.enter_context(nc.Block())

        @block.sync
        def _(sp):
            def x_transposed(n, half, c0, c1):
                sp.dma_start(xt_stage(half, c0, c1), xT[half].rearrange("p (k n) -> p k n", k=KC)[:, :, c0 * S:c1 * S]
                             ).then_inc(s_xt[n], 16)

            sp.dma_start(cin[:], ints[:, :]).then_inc(s_ints, 16)
            sp.dma_start(cst[:], consts[:, :]).then_inc(s_cst, 16)
            x_transposed(0, 0, 0, 2)
            for k in range(KC):
                sp.dma_start(wrw[:, k, :], wqkv[0].rearrange("p (k n) -> p k n", k=KC)[:, k, :]).then_inc(s_w0[k], 16)
            sp.dma_start(kpos_stage, kpos[:, :]).then_inc(s_tables, 16)
            sp.dma_start(nw[:].rearrange("p h d -> p (h d)"), normw[:, :]).then_inc(s_tables, 16)
            x_transposed(1, 0, 2, 4)
            x_transposed(2, 1, 0, 4)
            sp.dma_start(wo_raw[:], wo[0]).then_inc(s_woraw, 16)
            for half in range(2):
                sp.wait_ge(d_xlo, (half + 1) * HB)
                sp.dma_start(y[:, half * HB:(half + 1) * HB, :], x[half * HB:(half + 1) * HB].rearrange("b s h -> s b h")
                             ).then_inc(s_y[half], 16)

            def next_weights(h):
                sp.wait_ge(d_wlo, h * SPLITS)
                sp.dma_start(w_raw[:], wqkv[h]).then_inc(s_wraw, 16)
                sp.wait_ge(d_wolo, h * 4)
                sp.dma_start(wo_raw[:], wo[h]).then_inc(s_woraw, 16)

            with sp.Fori(1, HK) as h:
                next_weights(h)
            sp.wait_ge(d_wlo, HK * SPLITS)
            sp.dma_start(w_raw[:, 0:KC * WL], w1[:, :]).then_inc(s_wraw, 16)
            sp.wait_ge(d_wolo, HK * 4)
            sp.dma_start(wo_raw[:, 0:HID], wB[:, :]).then_inc(s_woraw, 16)
            for b in range(B):
                sp.wait_ge(d_fin, b + 1)
                sp.dma_start(out[b], y[:, b, :]).then_inc(s_out, 16)
            sp.wait_ge(s_out, 16 * B)

        @block.gpsimd
        def _(pool):
            nc.gpsimd.memset(mhalf[:], -0.5).then_inc(p_init, 1)
            nc.gpsimd.memset(top[:], 0.0).then_inc(p_init, 1)

            def gather(b):
                pool.wait_ge(d_rows, 1)
                nc.gpsimd.tensor_scalar(rows[:, b % B, :], rows[:, b % B, :], float(PAGES * PSIZE), None,
                                        ALU.add).then_inc(p_rows, 1)

            def gather_dma(i, b):
                wait(pool, p_rows, i, b)
                wait(pool, pe_ktc, i, b - 2)
                wait(pool, p_v, i, b - 2, 2)
                carry(pool, i, p_mark)
                for t in range(CT):
                    pool.indirect_dma_start(kv_raw[:, b % 2, t, :], None, kv[:, :],
                                            bass.IndirectOffsetOnAxis(rows[:, b % B, t:t + 1], 0)
                                            ).then_inc(s_kv[b % 2], 16)

            def step(i, b):
                g1 = b + 1
                if has(i, g1):
                    wait(pool, d_ss, i, g1)
                    carry(pool, i, p_mark)
                    nc.gpsimd.tensor_scalar(meansq[:], sumsq[:], 1.0 / D, NORM_EPS, ALU.mult, ALU.add).then_inc(p_ms, 1)
                    wait(pool, p_ms, i, g1)
                    nc.gpsimd.tensor_tensor(rstd[:], meansq[:], mhalf[:], ALU.pow).then_inc(p_rstd, 1)
                    wait(pool, p_rstd, i, g1)
                    wait(pool, d_u, i, g1 - 1)
                    nc.gpsimd.tensor_tensor(wr[:], nw[:], rstd[:].unsqueeze(2).to_broadcast([P, NH, D]),
                                            ALU.mult).then_inc(p_wr, 1)
                    wait(pool, d_u, i, g1)
                    wait(pool, pe_ktn, i, g1 - 1)
                    if first_keys(i, b):
                        pool.wait_ge(a_sincos, 2)
                    nc.gpsimd.tensor_tensor(rot[:].rearrange("p h (t d) -> p (h t) d", t=2),
                                            u[:].rearrange("p h (t d) -> p (h t) d", t=2),
                                            cos[:, g1 % B, :].unsqueeze(1).to_broadcast([P, 2 * NH, HALF]),
                                            ALU.mult).then_inc(p_m1, 1)
                    wait(pool, p_m1, i, g1)
                    wait(pool, d_m2, i, g1)
                    for a, c in ((0, HALF), (HALF, 0)):
                        nc.gpsimd.tensor_tensor(rot[:, :, a:a + HALF], rot[:, :, a:a + HALF],
                                                m2[:, :, c:c + HALF], ALU.add).then_inc(p_rot, 1)
                if has(i, b):
                    cached, new = kv_raw[:, b % 2, :, D:2 * D], raw[:, b % 2, QW + D:WW]
                    wait(pool, a_vhi, i, b, 2)
                    nc.gpsimd.tensor_tensor(v_lo[:, 0:CT, :], cached, v_hi[:, 0:CT, :].bitcast(F32), ALU.subtract).then_inc(p_v, 1)
                    nc.gpsimd.tensor_tensor(v_lo[:, CT, :], new, v_hi[:, CT, :].bitcast(F32), ALU.subtract).then_inc(p_v, 1)
                    if has(i, b + 2):
                        gather(b + 2)
                        gather_dma(i, b + 2)

            pool.wait_ge(d_rows, 1)
            for b in range(2):
                gather(b)
            for b in range(2):
                gather_dma(0, b)
            pool.wait_ge(s_tables, 32)
            pool.wait_ge(p_init, 2)
            for b in range(-2, B):
                step(0, b)
            with pool.Fori(B, G - B, B) as i:
                for b in range(B):
                    step(i, b)
            for b in range(B + 1):
                step(G - B, b)

        @block.scalar
        def _(act):
            def split_w(k0, k1, c0, c1):
                nc.scalar.activation(wh[:, k0:k1, c0:c1], wrw[:, k0:k1, c0:c1], ACT.Copy).then_inc(a_whi, 1)

            def split_wo(h):
                c = slice(h * HID, (h + 1) * HID)
                nc.scalar.activation(wo_hi[:, c], wo_raw[:, c], ACT.Copy).then_inc(a_wohi, 1)

            def split_x(b):
                half, c = b // HB, b % HB
                if b == 0 or b == 2 or b == HB:
                    act.wait_ge(s_xt[(b > 0) + (b > 2)], 16)
                nc.scalar.activation(xt_hi[:, :, b * S:(b + 1) * S], xt_stage(half, c, c + 1), ACT.Copy).then_inc(a_xhi, 1)

            def expert_products(b):
                act.wait_ge(pe_ar, b + 1)
                act.wait_ge(d_lg, b + 1)
                if b < B - 1:
                    act.wait_ge(d_base, 2 * b + 1)
                nc.scalar.activation(hflat[:, b * ER:(b + 1) * ER], expert_bank(b)[:, 0:ER], ACT.Copy).then_inc(a_h, 1)

            def sines():
                act.wait_ge(d_ang, 1)
                ang = ps[:, 0, 0:B * HALF].rearrange("p (b d) -> p b d", b=B)
                absang = ps[:, 1, 0:B * HALF].rearrange("p (b d) -> p b d", b=B)
                nc.scalar.activation(sin[:, :, 0:HALF], ang, ACT.Sin).then_inc(a_sincos, 1)
                nc.scalar.activation(cos[:], absang, ACT.Sin, bias=halfpi[:, 0:1], scale=-1.0).then_inc(a_sincos, 1)
                act.wait_ge(a_table, 1)
                nc.scalar.activation(unused[:], mhalf[:, 0:1], ACT.Exp).then_inc(a_table, 1)

            def turn_x(i, b, unit):
                c = turned(i, b, unit)
                if c is not None:
                    act.wait_ge(pe_xt, c + 1)
                    nc.scalar.activation(xt_hi[:, :, c * S:(c + 1) * S], bank(unit).rearrange("p (k s) -> p k s", k=KC),
                                         ACT.Copy).then_inc(a_xhi, 1)

            def step(i, b):
                g1, g2 = b + 1, b + 2
                last_head = isinstance(i, int) and i == G - B

                def exps(h):
                    wait(act, d_max, i, b, 4, h + 1)
                    nc.scalar.activation(ps[:, h, :], ps[:, h, :], ACT.Exp, bias=negmax[:, b % 2, h:h + 1], scale=-1.0,
                                         accum_out=rowsum[:, b % 2, h:h + 1]).then_inc(a_exp, 1)

                def norm(h):
                    wait(act, d_recip, i, b, 4, h + 1)
                    nc.scalar.activation(ps[:, h, :], ps[:, h, :], ACT.Copy, scale=recip[:, b % 2, h:h + 1]).then_inc(a_norm, 1)

                def probs(h):
                    wait(act, pe_t, i, b, 4, h + 1)
                    nc.scalar.activation(pt_hi[:, 0:CT, h, :], bank(f"T{h}").rearrange("p (t q) -> p t q", t=CT),
                                         ACT.Copy).then_inc(a_pt, 1)

                def cached_keys():
                    wait(act, pe_ktc, i, g1)
                    nc.scalar.activation(kt_hi[:, 0:L], bank("KTC"), ACT.Copy).then_inc(a_ktc, 1)

                def query_weights(k):
                    if has(i, B):
                        if k == 0:
                            wait(act, pe_q, i, B - 1)
                            act.wait_ge(s_wraw, i * 2 + 16)
                        split_w(k, k + 1, 0, QW)

                def second_layer_weights(k):
                    if last_head:
                        if k == 0:
                            wait(act, pe_kv, i, B - 1)
                            act.wait_ge(s_wraw, 16 * HK)
                        nc.scalar.activation(w_hi[:, k * WL:(k + 1) * WL], w_raw[:, k * WL:(k + 1) * WL], ACT.Copy).then_inc(a_whi, 1)

                def output_weights(h):
                    if h == 0:
                        wait(act, pe_y, i, -1)
                        act.wait_ge(s_woraw, i * 2 + 16)
                    split_wo(h)

                if has(i, g1):
                    wait(act, pe_kv, i, g1)
                    wait(act, p_v, i, g1 - 2, 2)
                    nc.scalar.activation(raw[:, g1 % 2, QW:WW], bank("KV")[:, 0:2 * D], ACT.Copy).then_inc(a_kv, 1)
                    wait(act, a_kv, i, g1)
                    wait(act, a_q, i, g1)
                    wait(act, d_m2, i, g1 - 1)
                    wait(act, p_m1, i, g1 - 1)
                    nc.scalar.activation(u[:].rearrange("p h d -> p (h d)"), raw[:, g1 % 2, 0:QW + D], ACT.Square).then_inc(a_sq, 1)
                if first_keys(i, b):
                    sines()
                if b == B - 1:
                    second_layer_weights(2)
                if b == 1:
                    output_weights(2)
                if b == B - 2:
                    query_weights(3)
                    second_layer_weights(0)
                if has(i, b):
                    exps(0)
                    norm(0)
                    exps(1)
                    norm(1)
                if b == B - 2 and has(i, B):
                    wait(act, pe_kv, i, B - 1)
                    split_w(0, KC // 2, QW, WW)
                if last_step(i, b):
                    expert_products(0)
                if has(i, b - 1):
                    wait(act, pe_o, i, b - 1)
                    wait(act, pe_y, i, b - 2)
                    nc.scalar.activation(o_hi[:], bank("O"), ACT.Copy).then_inc(a_o, 1)
                if last_step(i, b):
                    act.wait_ge(pe_s, 4 * G)
                    act.wait_ge(s_woraw, 16 * (HK + 1))
                    nc.scalar.activation(kt_hi[:, 0:HID], wo_raw[:, 0:HID], ACT.Copy).then_inc(a_wohi, 1)
                    expert_products(1)
                    expert_products(2)
                if has(i, b):
                    probs(0)
                    wait_kv(act, i, b)
                    wait(act, a_kv, i, b)
                    wait(act, pe_o, i, b - 1)
                    nc.scalar.activation(v_hi[:, 0:CT, :], kv_raw[:, b % 2, :, D:2 * D], ACT.Copy).then_inc(a_vhi, 1)
                    nc.scalar.activation(v_hi[:, CT, :], raw[:, b % 2, QW + D:WW], ACT.Copy).then_inc(a_vhi, 1)
                    exps(2)
                    norm(2)
                if has(i, g2):
                    wait(act, pe_q, i, g2)
                    wait(act, d_u, i, g2 - 2)
                    if isinstance(i, int) and i == 0 and g2 == 1:
                        act.wait_ge(d_mask, B)
                    nc.scalar.activation(raw[:, g2 % 2, 0:QW], bank("Q"), ACT.Copy).then_inc(a_q, 1)
                turn_x(i, b, "Q")
                if b == 1:
                    output_weights(3)
                if b == B - 3:
                    query_weights(0)
                if b == B - 2 and has(i, B):
                    split_w(KC // 2, KC, QW, WW)
                if b == B - 1:
                    second_layer_weights(3)
                if b >= 0:
                    for c in first_steps_x(i, b):
                        split_x(c)
                if has(i, b):
                    probs(1)
                    exps(3)
                    norm(3)
                    probs(2)
                if first_keys(i, b):
                    cached_keys()
                if has(i, g1):
                    wait(act, pe_qt, i, g1)
                    nc.scalar.activation(qt_hi[:], bank("QT"), ACT.Copy).then_inc(a_qt, 1)
                    if not first_keys(i, b):
                        cached_keys()
                if b == 0:
                    output_weights(0)
                if b == B - 3:
                    query_weights(1)
                if has(i, g1):
                    wait(act, pe_ktn, i, g1)
                    nc.scalar.activation(kt_hi[:, L:KEYS], bank("KTN")[:, 0:S], ACT.Copy).then_inc(a_ktn, 1)
                for unit in ("QT", "KTC", "KV", "KTN"):
                    turn_x(i, b, unit)
                if has(i, b):
                    probs(3)
                    wait(act, pe_tn, i, b)
                    nc.scalar.activation(pt_hi[:, CT, :, :].rearrange("p h q -> p (h q)"), bank("TN"), ACT.Copy).then_inc(a_pt, 1)
                if b == 0:
                    output_weights(1)
                if b == B - 3:
                    query_weights(2)
                if first_keys(i, b):
                    for c in first_steps_x(i, b):
                        split_x(c)
                if b == B - 2:
                    second_layer_weights(1)

            act.wait_ge(p_init, 2)
            nc.scalar.activation(unused[:], mhalf[:, 0:1], ACT.Sin).then_inc(a_table, 1)
            split_x(0)
            split_x(1)
            for k in range(KC):
                act.wait_ge(s_w0[k], 16)
                split_w(k, k + 1, 0, QW)
            split_w(0, KC // 2, QW, WW)
            split_w(KC // 2, KC, QW, WW)
            for b in range(-2, B):
                step(0, b)
            with act.Fori(B, G - B, B) as i:
                for b in range(B):
                    step(i, b)
            for b in range(B + 1):
                step(G - B, b)

            def second_expert(c):
                act.wait_ge(d_gd, c + 1)
                nc.scalar.activation(ge[:, c * HB:(c + 1) * HB], gd[:, c * HB:(c + 1) * HB], ACT.Exp).then_inc(a_ge, 1)

            def gated(c):
                act.wait_ge(pe_ht, c + 1)
                nc.scalar.activation(pt_hi[:, c, :, :].rearrange("p h q -> p (h q)"), ps_w[:, c, :], ACT.Copy).then_inc(a_ht, 1)

            expert_products(3)
            act.wait_ge(pe_xt, B)
            nc.scalar.activation(xt_hi[:, :, (B - 1) * S:B * S], ps_w[:, 0, :].rearrange("p (k s) -> p k s", k=KC),
                                 ACT.Copy).then_inc(a_xhi, 1)
            second_expert(0)
            for b in range(HB, B - 2):
                expert_products(b)
            gated(0)
            for b in range(B - 2, B):
                expert_products(b)
            second_expert(1)
            gated(1)

        @block.vector
        def _(dve):
            def low(out_ap, full, hi):
                return nc.vector.tensor_tensor(out_ap, full, hi.bitcast(F32), ALU.subtract)

            def split_w(k0, k1, c0, c1):
                low(wl[:, k0:k1, c0:c1], wrw[:, k0:k1, c0:c1], wh[:, k0:k1, c0:c1]).then_inc(d_wlo, 1)

            def split_wo(i, h):
                dve.wait_ge(a_wohi, (i >> 1) + (h + 1))
                c = slice(h * HID, (h + 1) * HID)
                low(wo_lo[:, c], wo_raw[:, c], wo_hi[:, c]).then_inc(d_wolo, 1)

            def split_x(b):
                half, c = b // HB, b % HB
                dve.wait_ge(a_xhi, b + 1)
                low(xt_lo[:, :, b * S:(b + 1) * S], xt_stage(half, c, c + 1), xt_hi[:, :, b * S:(b + 1) * S]).then_inc(d_xlo, 1)

            def masks(b0, b1):
                for b in range(b0, b1):
                    nc.vector.tensor_scalar(mask[:, b, :], kpos_stage, lenf[:, b:b + 1], MASKED, ALU.is_ge,
                                            ALU.mult).then_inc(d_mask, 1)

            def biases():
                for b in range(B):
                    nc.vector.tensor_scalar(lang_bias[:, b, :], cst[:, C_EXPERT:C_ROW], langf[:, b:b + 1], LANG_BIAS,
                                            ALU.is_equal, ALU.mult).then_inc(d_bias, 1)

            def biased(b):
                dve.wait_ge(pe_ar, b + 1)
                nc.vector.tensor_tensor(logits[:, b, :], expert_bank(b)[:, ER:ER + E], lang_bias[:, b, :],
                                        ALU.add).then_inc(d_lg, 1)

            def add_base(b):
                for product, cols in base_banks(b):
                    nc.vector.tensor_tensor(y[:, b, cols], product, y[:, b, cols], ALU.add).then_inc(d_base, 1)

            def turn_x(i, b, unit):
                c = turned(i, b, unit)
                if c is not None:
                    dve.wait_ge(a_xhi, B + c + 1)
                    low(xt_lo[:, :, c * S:(c + 1) * S], bank(unit).rearrange("p (k s) -> p k s", k=KC),
                        xt_hi[:, :, c * S:(c + 1) * S]).then_inc(d_xlo, 1)

            def step(i, b):
                g1 = b + 1
                last_head = isinstance(i, int) and i == G - B

                def halves(keys):
                    return keys.rearrange("p (c k) -> p c k", c=2)

                def rowmax(h):
                    wait(dve, pe_s, i, b, 4, h + 1)
                    wait(dve, pe_tn, i, b - 1)
                    carry(dve, i, d_mark)
                    nc.vector.tensor_tensor_reduce(out=halves(ps[:, h, :]), in0=ps_s[:, h % 2, :, 0:KH], in1=halves(mask[:, b % B, :]),
                                                   scale=-SCALE, scalar=3.0e38, op0=ALU.add, op1=ALU.min,
                                                   accum_out=negmax[:, b % 2, h:h + 1]).then_inc(d_max, 1)

                def over_sum(h):
                    wait(dve, a_exp, i, b, 4, h + 1)
                    wait(dve, a_norm, i, b - 2, 4)
                    nc.vector.reciprocal(recip[:, b % 2, h:h + 1], rowsum[:, b % 2, h:h + 1]).then_inc(d_recip, 1)

                def probs(h):
                    wait(dve, a_pt, i, b, 5, h + 1)
                    low(pt_lo[:, 0:CT, h, :], bank(f"T{h}").rearrange("p (t q) -> p t q", t=CT),
                        pt_hi[:, 0:CT, h, :]).then_inc(d_pt, 1)

                def cached_keys():
                    wait(dve, a_ktc, i, g1)
                    low(kt_lo[:, 0:L], bank("KTC"), kt_hi[:, 0:L]).then_inc(d_ktc, 1)

                def query_weights(k):
                    if has(i, B):
                        dve.wait_ge(a_whi, next_split(i, k))
                        split_w(k, k + 1, 0, QW)

                def key_value_weights(c):
                    if has(i, B):
                        dve.wait_ge(a_whi, next_split(i, KC + c))
                        split_w(c * KC // 2, (c + 1) * KC // 2, QW, WW)

                def second_layer_weights(k):
                    if last_head:
                        dve.wait_ge(a_whi, SPLITS * HK + k + 1)
                        c = slice(k * WL, (k + 1) * WL)
                        low(w_lo[:, c], w_raw[:, c], w_hi[:, c]).then_inc(d_wlo, 1)

                if isinstance(i, int) and i == 0 and b == 0:
                    dve.wait_ge(d_mask, B)
                if has(i, b):
                    rowmax(0)
                    rowmax(1)
                    over_sum(0)
                if has(i, g1):
                    wait(dve, a_sq, i, g1)
                    wait(dve, p_rstd, i, g1 - 1)
                    nc.vector.tensor_reduce(sumsq[:], u[:], AX_X, ALU.add).then_inc(d_ss, 1)
                if first_keys(i, b):
                    dve.wait_ge(s_tables, 32)
                    masks(0, B - 2)
                    dve.wait_ge(a_sincos, 2)
                    nc.vector.tensor_scalar(sin[:, :, HALF:D], sin[:, :, 0:HALF], -1.0, None, ALU.mult).then_inc(d_tab, 1)
                    dve.wait_ge(d_tab, 1)
                if b == B - 1:
                    second_layer_weights(2)
                if b == 1:
                    split_wo(i, 2)
                if b == B - 2:
                    query_weights(3)
                    second_layer_weights(0)
                if has(i, b):
                    over_sum(1)
                if b == B - 2:
                    key_value_weights(0)
                if last_step(i, b):
                    dve.wait_ge(d_bias, B)
                    biased(0)
                    add_base(0)
                if has(i, b - 1):
                    wait(dve, a_o, i, b - 1)
                    low(o_lo[:], bank("O"), o_hi[:]).then_inc(d_olo, 1)
                if last_step(i, b):
                    dve.wait_ge(a_wohi, 4 * HK + 1)
                    low(kt_lo[:, 0:HID], wo_raw[:, 0:HID], kt_hi[:, 0:HID]).then_inc(d_wolo, 1)
                    for c in (1, 2):
                        biased(c)
                        add_base(c)
                if has(i, b):
                    rowmax(2)
                if has(i, g1):
                    wait(dve, p_wr, i, g1)
                    wait(dve, d_ss, i, g1)
                    nc.vector.tensor_tensor(u[:].rearrange("p h d -> p (h d)"), raw[:, g1 % 2, 0:QW + D],
                                            wr[:].rearrange("p h d -> p (h d)"), ALU.mult).then_inc(d_u, 1)
                if has(i, b):
                    over_sum(2)
                if has(i, g1):
                    wait(dve, d_u, i, g1)
                    wait(dve, p_rot, i, g1 - 1, 2)
                    nc.vector.tensor_tensor(m2[:], u[:], sin[:, g1 % B, :].unsqueeze(1).to_broadcast([P, NH, D]),
                                            ALU.mult).then_inc(d_m2, 1)
                if first_keys(i, b):
                    masks(B - 2, B)
                    biases()
                if has(i, b):
                    rowmax(3)
                    probs(0)
                if b == 1:
                    split_wo(i, 3)
                if b == B - 3:
                    query_weights(0)
                if b == B - 2:
                    key_value_weights(1)
                turn_x(i, b, "Q")
                if b == B - 1:
                    second_layer_weights(3)
                if b >= 0:
                    for c in first_steps_x(i, b):
                        split_x(c)
                if has(i, b):
                    probs(1)
                    over_sum(3)
                if isinstance(i, int) and i == 0 and b > 0 and (b - 1) % HB == 0:
                    dve.wait_ge(s_y[(b - 1) // HB], 16)
                if has(i, b - 1):
                    wait(dve, pe_y, i, b - 1)
                    yb = y[:, (b - 1) % B, :]
                    nc.vector.tensor_tensor(yb, bank("Y"), yb, ALU.add).then_inc(d_y, 1)
                if has(i, b):
                    probs(2)
                if first_keys(i, b):
                    cached_keys()
                if has(i, g1):
                    wait(dve, a_qt, i, g1)
                    low(qt_lo[:], bank("QT"), qt_hi[:]).then_inc(d_qt, 1)
                    if not first_keys(i, b):
                        cached_keys()
                    wait(dve, a_ktn, i, g1)
                    low(kt_lo[:, L:KEYS], bank("KTN")[:, 0:S], kt_hi[:, L:KEYS]).then_inc(d_ktn, 1)
                if b == 0:
                    split_wo(i, 0)
                if b == B - 3:
                    query_weights(1)
                for unit in ("QT", "KTC", "KV", "KTN"):
                    turn_x(i, b, unit)
                if has(i, b):
                    probs(3)
                    wait(dve, a_pt, i, b, 5)
                    low(pt_lo[:, CT, :, :].rearrange("p h q -> p (h q)"), bank("TN"),
                        pt_hi[:, CT, :, :].rearrange("p h q -> p (h q)")).then_inc(d_pt, 1)
                if b == 0:
                    split_wo(i, 1)
                if b == B - 3:
                    query_weights(2)
                if first_keys(i, b):
                    for c in first_steps_x(i, b):
                        split_x(c)
                if b == B - 2:
                    second_layer_weights(1)

            n_tab = [0]

            def tab(ins):
                ins.then_inc(d_gate, 1)
                n_tab[0] += 1
                dve.wait_ge(d_gate, n_tab[0])

            dve.wait_ge(s_ints, 16)
            tab(nc.vector.tensor_copy(blkf[:].rearrange("p b t -> p (b t)"), cin[:, I_BLOCK:I_LEN]))
            dve.wait_ge(s_cst, 16)
            tab(nc.vector.tensor_scalar(blkf[:], blkf[:], float(PSIZE), cst[:, C_SLOT:C_SLOT + 1], ALU.mult, ALU.add))
            nc.vector.tensor_scalar(rows[:], blkf[:], -float(PAGES * PSIZE), None, ALU.add).then_inc(d_rows, 1)
            tab(nc.vector.memset(halfpi[:], float(np.pi / 2)))
            tab(nc.vector.tensor_copy(lenf[:], cin[:, I_LEN:I_LANG]))
            tab(nc.vector.tensor_scalar(pos[:], lenf[:], cst[:, C_ROW:C_ROW + 1], None, ALU.add))
            ang = ps[:, 0, 0:B * HALF].rearrange("p (b d) -> p b d", b=B)
            absang = ps[:, 1, 0:B * HALF].rearrange("p (b d) -> p b d", b=B)
            turns = ps[:, 2, 0:B * HALF].rearrange("p (b d) -> p b d", b=B)
            whole = ps[:, 3, 0:B * HALF].bitcast(I32).rearrange("p (b d) -> p b d", b=B)
            tab(nc.vector.tensor_tensor(ang, cst[:, C_INVF:C_INVF + HALF].unsqueeze(1).to_broadcast([P, B, HALF]),
                                        pos[:].unsqueeze(2).to_broadcast([P, B, HALF]), ALU.mult))
            tab(nc.vector.tensor_scalar(whole, ang, float(1.0 / TWO_PI), None, ALU.mult))
            tab(nc.vector.tensor_copy(turns, whole))

            def query_weights(k):
                dve.wait_ge(a_whi, k + 1)
                split_w(k, k + 1, 0, QW)

            split_x(0)
            split_x(1)
            for k in range(KC):
                query_weights(k)
            for c in range(2):
                dve.wait_ge(a_whi, KC + c + 1)
                split_w(c * KC // 2, (c + 1) * KC // 2, QW, WW)
            for part in (TWO_PI_A, TWO_PI_B, TWO_PI_C):
                tab(nc.vector.scalar_tensor_tensor(out=ang, in0=turns, scalar=-part, in1=ang, op0=ALU.mult, op1=ALU.add))
            tab(nc.vector.tensor_scalar(ang, ang, PI_BELOW, -PI_BELOW, ALU.min, ALU.max))
            nc.vector.scalar_tensor_tensor(out=absang, in0=ang, scalar=-1.0, in1=ang, op0=ALU.mult, op1=ALU.max).then_inc(d_ang, 1)
            tab(nc.vector.tensor_copy(langf[:], cin[:, I_LANG:I_END]))
            for b in range(-2, B):
                step(0, b)
            with dve.Fori(B, G - B, B) as i:
                for b in range(B):
                    step(i, b)
            for b in range(B + 1):
                step(G - B, b)

            def largest(b):
                dve.wait_ge(d_lg, b + 1)
                nc.vector.max(out=top[:, b, 0:8], in_=logits[:, b, :]).then_inc(d_gate, 1)
                n_tab[0] += 1

            def gates(c):
                half = slice(c * HB, (c + 1) * HB)
                batches = range(c * HB, (c + 1) * HB)

                def first_index(n, values):
                    for b in batches:
                        nc.vector.max_index(out=topi[:, n, b, :], in_max=top[:, b, n:n + 8], in_values=values[:, b, :]).then_inc(d_gate, 1)
                    n_tab[0] += HB
                    dve.wait_ge(d_gate, n_tab[0])
                    tab(nc.vector.tensor_copy(topf[:, n, half].unsqueeze(2), topi[:, n, half, 0:1]))
                    tab(nc.vector.tensor_tensor(gate[:, n, half, :], cst[:, C_EXPERT:C_ROW].unsqueeze(1).to_broadcast([P, HB, E]),
                                                topf[:, n, half].unsqueeze(2).to_broadcast([P, HB, E]), ALU.is_equal))

                dve.wait_ge(d_gate, n_tab[0])
                nc.vector.tensor_tensor(gd[:, half].unsqueeze(2), top[:, half, 1:2], top[:, half, 0:1], ALU.subtract).then_inc(d_gd, 1)
                first_index(0, logits)
                tab(nc.vector.scalar_tensor_tensor(out=others[:, half, :], in0=gate[:, 0, half, :], scalar=MASKED, in1=logits[:, half, :],
                                                   op0=ALU.mult, op1=ALU.add))
                first_index(1, others)
                dve.wait_ge(a_ge, c + 1)
                tab(nc.vector.tensor_scalar(gs[:, half], ge[:, half], 1.0, None, ALU.add))
                tab(nc.vector.reciprocal(gd[:, half], gs[:, half]))
                tab(nc.vector.tensor_scalar(gw[:, 0, half], gd[:, half], LORA_SCALING, None, ALU.mult))
                tab(nc.vector.tensor_tensor(gw[:, 1, half], gw[:, 0, half], ge[:, half], ALU.mult))
                for n in range(2):
                    tab(nc.vector.tensor_tensor(gate[:, n, half, :], gate[:, n, half, :],
                                                gw[:, n, half].unsqueeze(2).to_broadcast([P, HB, E]), ALU.mult))
                tab(nc.vector.tensor_tensor(gate[:, 0, half, :], gate[:, 0, half, :], gate[:, 1, half, :], ALU.add))
                dve.wait_ge(a_h, (c + 1) * HB)
                hh = hflat[:, c * HB * ER:(c + 1) * HB * ER].rearrange("p (e r) -> p e r", r=R)
                nc.vector.tensor_tensor(hh, hh, gate[:, 0, half, :].rearrange("p b e -> p (b e)").unsqueeze(2).to_broadcast([P, HB * E, R]),
                                        ALU.mult).then_inc(d_hg, 1)

            def gated(c):
                dve.wait_ge(a_ht, c + 1)
                low(pt_lo[:, c, :, :].rearrange("p h q -> p (h q)"), ps_w[:, c, :],
                    pt_hi[:, c, :, :].rearrange("p h q -> p (h q)")).then_inc(d_ht, 1)

            def add_experts(b):
                dve.wait_ge(pe_out, b + 1)
                nc.vector.tensor_tensor(y[:, b, :], result_bank(b), y[:, b, :], ALU.add).then_inc(d_fin, 1)

            dve.wait_ge(p_init, 2)
            for b in range(HB - 1):
                largest(b)
            biased(3)
            largest(3)
            add_base(3)
            dve.wait_ge(a_xhi, 2 * B)
            low(xt_lo[:, :, (B - 1) * S:B * S], ps_w[:, 0, :].rearrange("p (k s) -> p k s", k=KC),
                xt_hi[:, :, (B - 1) * S:B * S]).then_inc(d_xlo, 1)
            gates(0)
            for b in range(HB, B - 1):
                if b == B - 2:
                    gated(0)
                biased(b)
                add_base(b)
                largest(b)
            biased(B - 1)
            largest(B - 1)
            gates(1)
            add_experts(0)
            gated(1)
            for b in range(1, B):
                add_experts(b)

        @block.tensor
        def _(pe):
            def turn_x(i, b, unit):
                c = turned(i, b, unit)
                if c is None:
                    return
                wait(pe, d_y, i, c)
                wait_bank(pe, i, b, unit)
                for k in range(KC):
                    last = nc.tensor.transpose(bank(unit)[:, k * S:(k + 1) * S], y[:, c, k * P:(k + 1) * P], ident)
                last.then_inc(pe_xt, 1)

            w1h = w_hi[:, 0:KC * WL].rearrange("p (k n) -> p k n", k=KC)
            w1l = w_lo[:, 0:KC * WL].rearrange("p (k n) -> p k n", k=KC)

            def x_tiles(b, c0, c1):
                return [(xt_hi[:, k, b * S:(b + 1) * S], xt_lo[:, k, b * S:(b + 1) * S], w1h[:, k, c0:c1], w1l[:, k, c0:c1])
                        for k in range(KC)]

            def free_second_layer(b):
                pe.wait_ge(d_xlo, B + b + 1)
                if b < 2:
                    pe.wait_ge(d_max, 4 * G - 1 + b)
                else:
                    pe.wait_ge(a_h, b - 1)
                    pe.wait_ge(d_base, 2 * (b - 1))

            def second_layer(b):
                if b == 0:
                    pe.wait_ge(d_wlo, SPLITS * HK + KC)
                free_second_layer(b)
                for k, (a_hi, a_lo, b_hi, b_lo) in enumerate(x_tiles(b, 0, WL)):
                    for n, (a, w) in enumerate(((a_hi, b_hi), (a_hi, b_lo), (a_lo, b_hi))):
                        for half in range(2):
                            last = nc.tensor.matmul(ps_s[:, b % 2, half, 0:WLH], a, w[:, half * WLH:(half + 1) * WLH],
                                                    start=k == 0 and n == 0, stop=k == KC - 1 and n == 2)
                last.then_inc(pe_ar, 1)

            def step(i, b):
                g1, g2 = b + 1, b + 2
                tok = slice(g2 % B * S, (g2 % B + 1) * S)

                def scores(h):
                    if h == 0:
                        wait(pe, d_qt, i, b)
                        wait(pe, d_ktc, i, b)
                        wait(pe, d_ktn, i, b)
                    if h >= 2:
                        wait(pe, d_max, i, b, 4, h - 1)
                    else:
                        wait(pe, d_max, i, b - 1, 4, h + 3)
                    qh, ql = qt_hi[:, h * S:(h + 1) * S], qt_lo[:, h * S:(h + 1) * S]
                    for n, (a, c) in enumerate(((qh, kt_hi), (qh, kt_lo), (ql, kt_hi))):
                        for half in range(2):
                            last = nc.tensor.matmul(ps_s[:, h % 2, half, 0:KH], a, c[:, half * KH:(half + 1) * KH],
                                                    start=n == 0, stop=n == 2)
                    last.then_inc(pe_s, 1)

                def turn_cached_keys():
                    wait_kv(pe, i, g1)
                    wait_bank(pe, i, b, "KTC")
                    for t in range(CT):
                        last = nc.tensor.transpose(bank("KTC")[:, t * P:(t + 1) * P], kv_raw[:, g1 % 2, t, 0:D], ident)
                    last.then_inc(pe_ktc, 1)

                def project_keys_values():
                    if b == -2:
                        pe.wait_ge(d_wlo, SPLITS)
                    if g2 == B:
                        pe.wait_ge(d_wlo, next_split(i, SPLITS - 1))
                    wait_bank(pe, i, b, "KV")
                    three_passes(bank("KV")[:, 0:2 * D], [(xt_hi[:, k, tok], xt_lo[:, k, tok], wh[:, k, QW:WW], wl[:, k, QW:WW])
                                                          for k in range(KC)]).then_inc(pe_kv, 1)

                def turn_probs(h):
                    wait(pe, a_norm, i, b, 4, h + 1)
                    wait_bank(pe, i, b, f"T{h}")
                    for t in range(CT):
                        last = nc.tensor.transpose(bank(f"T{h}")[:, t * S:(t + 1) * S], ps[:, h, t * P:(t + 1) * P], ident)
                    last.then_inc(pe_t, 1)

                if has(i, b):
                    scores(0)
                    scores(1)
                if last_step(i, b):
                    second_layer(0)
                if has(i, b - 1):
                    wait(pe, d_pt, i, b - 1, 5)
                    wait(pe, p_v, i, b - 1, 2)
                    wait_bank(pe, i, b, "O")
                    three_passes(bank("O"), [(v_hi[:, t, :], v_lo[:, t, :],
                                              pt_hi[:, t, :, :].rearrange("p h q -> p (h q)"),
                                              pt_lo[:, t, :, :].rearrange("p h q -> p (h q)")) for t in range(KT)]
                                 ).then_inc(pe_o, 1)
                if last_step(i, b):
                    second_layer(1)
                    second_layer(2)
                if has(i, b):
                    scores(2)
                    turn_probs(0)
                if has(i, g2):
                    if isinstance(i, int) and i == 0:
                        pe.wait_ge(d_xlo, min(g2, B - 1) + 1)
                    wait_bank(pe, i, b, "Q")

                    def weights_split(k):
                        if b == -2:
                            pe.wait_ge(d_wlo, k + 1)
                        if g2 == B:
                            pe.wait_ge(d_wlo, next_split(i, k))

                    three_passes(bank("Q"), [(xt_hi[:, k, tok], xt_lo[:, k, tok], wh[:, k, 0:QW], wl[:, k, 0:QW])
                                             for k in range(KC)], before=weights_split).then_inc(pe_q, 1)
                turn_x(i, b, "Q")
                if has(i, b):
                    scores(3)
                    turn_probs(1)
                if has(i, b - 1):
                    wait(pe, d_olo, i, b - 1)
                    wait_bank(pe, i, b, "Y")

                    def output_weights_split(h):
                        if (b - 1) % B == 0:
                            pe.wait_ge(d_wolo, (i >> 1) + (h + 1))

                    three_passes(bank("Y"), [(o_hi[:, h * S:(h + 1) * S], o_lo[:, h * S:(h + 1) * S],
                                              wo_hi[:, h * HID:(h + 1) * HID], wo_lo[:, h * HID:(h + 1) * HID])
                                             for h in range(REP)], before=output_weights_split).then_inc(pe_y, 1)
                if has(i, b):
                    turn_probs(2)
                if first_keys(i, b):
                    project_keys_values()
                    turn_cached_keys()
                if has(i, g1):
                    wait(pe, p_rot, i, g1, 2)
                    wait_bank(pe, i, b, "QT")
                    for h in range(REP):
                        last = nc.tensor.transpose(bank("QT")[:, h * S:(h + 1) * S], rot[:, h, :], ident)
                    last.then_inc(pe_qt, 1)
                    if not first_keys(i, b):
                        turn_cached_keys()
                turn_x(i, b, "QT")
                turn_x(i, b, "KTC")
                if has(i, g2) and not first_keys(i, b):
                    project_keys_values()
                turn_x(i, b, "KV")
                if has(i, g1):
                    wait_bank(pe, i, b, "KTN")
                    nc.tensor.transpose(bank("KTN")[:, 0:S], rot[:, REP, :], ident).then_inc(pe_ktn, 1)
                turn_x(i, b, "KTN")
                if has(i, b):
                    turn_probs(3)
                    wait_bank(pe, i, b, "TN")
                    for h in range(REP):
                        last = nc.tensor.transpose(bank("TN")[:, h * S:(h + 1) * S], ps[:, h, L:KEYS], ident)
                    last.then_inc(pe_tn, 1)

            for b in range(-2, B):
                if b == -1:
                    pe.wait_ge(s_cst, 16)
                step(0, b)
            with pe.Fori(B, G - B, B) as i:
                for b in range(B):
                    step(i, b)
            for b in range(B + 1):
                step(G - B, b)

            second_layer(3)
            pe.wait_ge(d_y, G)
            for k in range(KC):
                last = nc.tensor.transpose(ps_w[:, 0, k * S:(k + 1) * S], y[:, B - 1, k * P:(k + 1) * P], ident)
            last.then_inc(pe_xt, 1)
            for b in range(HB, B - 2):
                second_layer(b)

            def turn_gated(c):
                pe.wait_ge(d_hg, c + 1)
                for j in range(HB):
                    b = c * HB + j
                    last = nc.tensor.transpose(ps_w[:, c, j * S:(j + 1) * S], hflat[:, b * ER:(b + 1) * ER], ident)
                last.then_inc(pe_ht, 1)

            def lora(b):
                c, j = b // HB, b % HB
                if j == 0:
                    pe.wait_ge(d_ht, c + 1)
                if b == 0:
                    pe.wait_ge(d_wolo, 4 * HK + 1)
                if b == 2:
                    pe.wait_ge(d_base, 2 * (B - 1))
                    pe.wait_ge(a_h, B - 1)
                if 4 <= b < B - 1:
                    pe.wait_ge(d_fin, b - 3)
                three_passes(result_bank(b), [(pt_hi[:, c, j, :], pt_lo[:, c, j, :], kt_hi[:, 0:HID], kt_lo[:, 0:HID])],
                             start=b < B - 1).then_inc(pe_out, 1)

            turn_gated(0)
            second_layer(B - 2)
            free_second_layer(B - 1)
            three_passes(expert_bank(B - 1), x_tiles(B - 1, HID, WL)).then_inc(pe_ar, 1)
            for b in range(HB):
                lora(b)
            last_base = x_tiles(B - 1, 0, HID)
            three_passes(result_bank(B - 1), last_base[0:KC // 2], stop=False)
            turn_gated(1)
            three_passes(result_bank(B - 1), last_base[KC // 2:KC], start=False, stop=False)
            for b in range(HB, B):
                lora(b)


def kernel(**inputs):
    import concourse.bacc as _bacc
    from concourse.bass_utils import run_bass_kernel_spmd as _run

    a = {k: np.asarray(v) for k, v in inputs.items()}
    rows = np.arange(P)

    def tiles(m):
        return m.reshape(KC, P, -1).transpose(1, 0, 2).reshape(P, -1)

    x = a["x"]
    xT = x.transpose(2, 0, 1).reshape(KC, P, 2, B * S // 2).transpose(2, 1, 0, 3).reshape(2, P, -1)
    q, k, v = (a["L0_cond_" + n].T for n in ("Wq", "Wk", "Wv"))
    wqkv = np.stack([tiles(np.concatenate([q[:, h * QW:(h + 1) * QW], k[:, h * D:(h + 1) * D], v[:, h * D:(h + 1) * D]], 1))
                     for h in range(HK)])
    wo = a["L0_cond_Wo"].T.reshape(HK, REP, D, HID).transpose(0, 2, 1, 3).reshape(HK, P, -1)
    kv = np.concatenate([a["L0_cond_k_cache"], a["L0_cond_v_cache"]], -1).transpose(2, 0, 1, 3).reshape(HK * PAGES * PSIZE, 2 * D)
    normw = np.broadcast_to(np.concatenate([a["L0_cond_q_norm_w"]] * REP + [a["L0_cond_k_norm_w"]]), (P, NH * D))
    w1 = tiles(np.concatenate([a["L1_cond_W"].T, a["L1_cond_A"].reshape(ER, HID).T, a["L1_cond_Wr"].T], 1))
    wB = a["L1_cond_B"].transpose(0, 2, 1).reshape(ER, HID)

    consts = np.zeros((P, C_END), np.float32)
    consts[:, C_INVF:C_IDENT] = np.float32(1) / (THETA ** (np.arange(0, D, 2) / D)).astype(np.float32)
    consts[:, C_IDENT:C_EXPERT] = np.eye(P)
    consts[:, C_EXPERT:C_ROW] = np.arange(E)
    consts[:, C_ROW] = rows
    consts[:, C_SLOT] = rows % PSIZE
    kpos = np.empty((P, KEYS), np.float32)
    kpos[:, 0:L] = np.arange(L)
    kpos[:, L:KEYS] = -2.0**32
    ints = np.empty((P, I_END), np.int32)
    pages = a["itok_Bx16_0_63"].reshape(B, CT, P // PSIZE)[:, :, rows // PSIZE]
    ints[:, I_BLOCK:I_LEN] = pages.transpose(2, 0, 1).reshape(P, B * CT)
    ints[:, I_LEN:I_LANG] = a["itok_B_207_1644"]
    ints[:, I_LANG:I_END] = a["itok_B_0_7"]

    arrays = {"xT": xT, "x": x, "wqkv": wqkv, "wo": wo, "kv": kv, "normw": normw, "kpos": kpos, "consts": consts, "ints": ints,
              "w1": w1, "wB": wB}
    arrays = {n: np.ascontiguousarray(m) for n, m in arrays.items()}
    nc = _bacc.Bacc("TRN2", target_bir_lowering=False, num_devices=1)
    args = {n: nc.dram_tensor(n, m.shape, mybir.dt.from_np(m.dtype), kind="ExternalInput").ap() for n, m in arrays.items()}
    out = nc.dram_tensor("out", (B, S, HID), F32, kind="ExternalOutput").ap()
    attention_lora(nc, *args.values(), out)
    r = _run(nc, [arrays], core_ids=[0])
    return r.results[0]["out"]
```
